# Optimizing a Trainium2 kernel written in Bass

```python
import numpy as np
import jax
import jax.numpy as jnp

def _softmax(x, axis=-1):
    return jax.nn.softmax(x, axis=axis)

def _gelu(x):
    return jax.nn.gelu(x, approximate=True)

def _silu(x):
    return jax.nn.silu(x)

def _sigmoid(x):
    return jax.nn.sigmoid(x)

def _layernorm(x, axis=-1, eps=1e-05):
    m = jnp.mean(x, axis=axis, keepdims=True)
    v = jnp.var(x, axis=axis, keepdims=True)
    return (x - m) / jnp.sqrt(v + eps)

def _scatter_add(tgt, idx, src, axis=0):
    return tgt.at[idx].add(src)

def _segment_sum(src, seg, n):
    return jax.ops.segment_sum(src, seg, n)
kernel_name = 'mk_seq_postln_d1_jaxref_r4_4be0c8'

def setup_inputs(seed: int=0):
    np.random.seed(seed)
    _w = jnp.asarray

    def _L0_attn_setup():
        import jax, jax.numpy as jnp
        import numpy as np
        D_MODEL = 256
        NHEAD = 16
        WIN = 128
        key = jax.random.key(seed)
        k0, k1, k2 = jax.random.split(key, 3)
        B, S = (4, 1024)
        x = jax.random.normal(k0, (B, S, D_MODEL), dtype=jnp.float32)
        Wqkv = jax.random.normal(k1, (D_MODEL, 3 * D_MODEL), dtype=jnp.float32) * 0.02
        bqkv = jnp.zeros((3 * D_MODEL,), dtype=jnp.float32)
        Wout = jax.random.normal(k2, (D_MODEL, D_MODEL), dtype=jnp.float32) * 0.02
        bout = jnp.zeros((D_MODEL,), dtype=jnp.float32)
        return {'x': x, 'Wqkv': Wqkv, 'bqkv': bqkv, 'Wout': Wout, 'bout': bout}
    _L0_attn_in = _L0_attn_setup()

    def _L0_ffn_setup():
        import jax, jax.numpy as jnp
        import numpy as np
        EPS = 1e-05

        def _quantize(W):
            gamma = jnp.mean(jnp.abs(W))
            return jnp.clip(jnp.round(W / (gamma + EPS)), -1.0, 1.0)
        key = jax.random.key(seed)
        k_x, k_w1, k_b1, k_w2, k_b2 = jax.random.split(key, 5)
        n_embd = 256
        d_ff = 4 * n_embd
        B, S = (4, 1024)
        bound1 = 1.0 / np.sqrt(n_embd)
        bound2 = 1.0 / np.sqrt(d_ff)
        x = jax.random.normal(k_x, (B, S, n_embd), dtype=jnp.float32)
        W1 = jax.random.uniform(k_w1, (d_ff, n_embd), jnp.float32, -bound1, bound1)
        b1 = jax.random.uniform(k_b1, (d_ff,), jnp.float32, -bound1, bound1)
        W2 = jax.random.uniform(k_w2, (n_embd, d_ff), jnp.float32, -bound2, bound2)
        b2 = jax.random.uniform(k_b2, (n_embd,), jnp.float32, -bound2, bound2)
        return {'x': x, 'W1': W1, 'b1': b1, 'W2': W2, 'b2': b2}
    _L0_ffn_in = _L0_ffn_setup()
    _d = {'L0_attn_x': _L0_attn_in['x'], 'L0_attn_Wqkv': _L0_attn_in['Wqkv'], 'L0_attn_bqkv': _L0_attn_in['bqkv'], 'L0_attn_Wout': _L0_attn_in['Wout'], 'L0_attn_bout': _L0_attn_in['bout'], 'L0_ffn_W1': _L0_ffn_in['W1'], 'L0_ffn_b1': _L0_ffn_in['b1'], 'L0_ffn_W2': _L0_ffn_in['W2'], 'L0_ffn_b2': _L0_ffn_in['b2']}
    _x0 = _d['L0_attn_x']
    _d['L0_attn_x'] = jax.random.normal(jax.random.fold_in(jax.random.key(seed), 1), (16, 512, 256), dtype=_x0.dtype)
    del _x0
    return _d

def reference(L0_attn_x, L0_attn_Wqkv, L0_attn_bqkv, L0_attn_Wout, L0_attn_bout, L0_ffn_W1, L0_ffn_b1, L0_ffn_W2, L0_ffn_b2):

    def _L0_attn_ref(x, Wqkv, bqkv, Wout, bout):
        import jax, jax.numpy as jnp
        import numpy as np
        D_MODEL = 256
        NHEAD = 16
        WIN = 128
        B, S, dm = x.shape
        H, W = (NHEAD, WIN)
        Dh = dm // H
        nb = S // W
        qkv = (x @ Wqkv + bqkv).reshape(B, S, 3, H, Dh)
        q = qkv[:, :, 0].transpose(0, 2, 1, 3)
        k = qkv[:, :, 1].transpose(0, 2, 1, 3)
        v = qkv[:, :, 2].transpose(0, 2, 1, 3)
        qb = q.reshape(B, H, nb, W, Dh)
        kb = k.reshape(B, H, nb, W, Dh)
        vb = v.reshape(B, H, nb, W, Dh)
        kp = jnp.pad(kb, ((0, 0), (0, 0), (1, 1), (0, 0), (0, 0)))
        vp = jnp.pad(vb, ((0, 0), (0, 0), (1, 1), (0, 0), (0, 0)))
        kwin = jnp.concatenate([kp[:, :, :-2], kp[:, :, 1:-1], kp[:, :, 2:]], axis=3)
        vwin = jnp.concatenate([vp[:, :, :-2], vp[:, :, 1:-1], vp[:, :, 2:]], axis=3)
        scale = jnp.float32(1.0 / np.sqrt(dm))
        scores = jnp.einsum('bhnqd,bhnkd->bhnqk', qb, kwin) * scale
        n = jnp.arange(nb)[:, None, None]
        i = jnp.arange(W)[None, :, None]
        j = jnp.arange(3 * W)[None, None, :]
        qpos = n * W + i
        kpos = n * W - W + j
        mask = (jnp.abs(kpos - qpos) <= W) & (kpos >= 0) & (kpos < S)
        scores = jnp.where(mask[None, None], scores, jnp.float32(-1e+30))
        attn = jax.nn.softmax(scores, axis=-1)
        out = jnp.einsum('bhnqk,bhnkd->bhnqd', attn, vwin)
        out = out.reshape(B, H, S, Dh).transpose(0, 2, 1, 3).reshape(B, S, dm)
        return out @ Wout + bout

    def _L0_ffn_ref(x, W1, b1, W2, b2):
        import jax, jax.numpy as jnp
        import numpy as np
        EPS = 1e-05

        def _quantize(W):
            gamma = jnp.mean(jnp.abs(W))
            return jnp.clip(jnp.round(W / (gamma + EPS)), -1.0, 1.0)
        Wq1 = _quantize(W1)
        Wq2 = _quantize(W2)
        h = jax.nn.relu(jnp.einsum('bsd,fd->bsf', x, Wq1) + b1)
        out = jnp.einsum('bsf,df->bsd', h, Wq2) + b2
        return out
    x = L0_attn_x
    x = _layernorm(x + _L0_attn_ref(x, L0_attn_Wqkv, L0_attn_bqkv, L0_attn_Wout, L0_attn_bout), axis=-1)
    x = _layernorm(x + _L0_ffn_ref(x, L0_ffn_W1, L0_ffn_b1, L0_ffn_W2, L0_ffn_b2), axis=-1)
    return x

_drawn_inputs = setup_inputs


def setup_inputs(seed=0):
    import zlib

    import numpy as np

    out = dict(_drawn_inputs(seed))
    spreads = {'L0_attn_bqkv': (0.0, 0.1), 'L0_attn_bout': (0.0, 0.1)}
    factors = {'L0_attn_Wqkv': 8.0, 'L0_ffn_b1': 21.92, 'L0_ffn_b2': 64.0}
    for name, (base, spread) in spreads.items():
        noise = np.random.default_rng([zlib.crc32(name.encode()), seed]).standard_normal(out[name].shape)
        drawn = base * np.exp(spread * noise) if base else spread * noise
        out[name] = jnp.asarray(drawn.astype(out[name].dtype))
    for name, factor in factors.items():
        out[name] = (out[name] * factor).astype(out[name].dtype)
    return out
```

```python
from contextlib import ExitStack

import concourse.bass as bass
from concourse import mybir

F32 = mybir.dt.float32
F32R = mybir.dt.float32r
BF16 = mybir.dt.bfloat16
ALU = mybir.AluOpType
ACT = mybir.ActivationFunctionType

P = 128
B, S, D = 16, 512, 256
H, DH, W = 16, 16, 128
FF = 1024
NB = S // W
KC = D // P
FC = FF // P
QUADS = H // 4
TB = S // P
EPS = 1e-5
SCALE = 1.0 / 16.0
MASKED = -1e30
POOL_CONSTANTS = 9

PCOL = {1: (0, 384, 0, 384), 2: (768, 384, 128, 384), 3: (1536, 512, 256, 256), 0: (1792, 512, 0, 256)}
PW = 2560

SIDE = [
    [[], ["xs"], ["pva"], ["pvb"], ["ut", ("qk", 0)], [("ot", 0), ("ot", 1), ("qk", 1)], [("op", 0), "nmt"], [("op", 1), "ln1", ("vp", 0)]],
    [[], ["x1"], ["pva"], ["pvb"], ["ut", ("x1t", 0), ("x1t", 1)], [("vp", 1), ("f1", 0, 0)], [("f1", 0, 1), "nmt"], [("f1", 0, 2), ("f1", 0, 3)]],
    [[("f2", 0)], [], ["pva"], ["pvb"], ["ut", ("f1", 1, 0), ("ln2", 0)], [("f1", 1, 1)], [("f1", 1, 2), "nmt"], [("f1", 1, 3), ("out", 0)]],
    [[("f2", 1)], [("qk", 2)], ["pva"], ["pvb"], ["ut", ("ln2", 1)], [], [("qk", 3), "nmt"], [("out", 1)]],
]
MAXES = [(0, 3), (3, 6), (6, 9), (9, 12), (12, 14), (14, 16), (16, 16), (16, 16)]

USES_BANK = {"ut", "qk", "ot", "op", "vp", "x1t", "f1", "f2", "nmt"}
POST = {"ot", "op", "ln1", "x1", "x1t", "f1", "f2", "ln2", "out"}
NEXT = {"xs", "qk", "vp"}


def name_of(step):
    return step if isinstance(step, str) else step[0]


def banks():
    out, n = {}, 0
    for v in range(4):
        for k in range(8):
            for step in SIDE[v][k]:
                if name_of(step) in USES_BANK:
                    out[(v, step)] = n % 2
                    n += 1
    assert n % 2 == 0
    return out


BANK = banks()


def stages(b):
    if b is None:
        return True, True, True
    return 0 <= b < B, 1 <= b <= B, b + 1 < B


def side(v, k, b):
    attn, post, nxt = stages(b)
    for step in SIDE[v][k]:
        name = name_of(step)
        if name in POST:
            if post:
                yield step, -1, None
        elif name in NEXT:
            if nxt:
                yield step, 1, None
        elif name == "nmt":
            if (v < 3 and attn) or (v == 3 and nxt):
                yield step, (0 if v < 3 else 1), (v + 1) % 4
        elif v == 0:
            if post:
                yield step, -1, 3
        elif attn:
            yield step, 0, v - 1


def max_quad(v, b):
    attn, _, nxt = stages(b)
    if v < 3:
        return (0, v + 1) if attn else None
    return (1, 0) if nxt else None


def steps(eng, step):
    step(-1, -1)
    step(0, 0)
    with eng.Fori(1, B - 1) as b:
        step(b, None)
    step(B - 1, B - 1)
    step(B, B)


def in_register(eng, count):
    if isinstance(count, int):
        return count
    reg = eng.alloc_register()
    eng.reg_mov(reg, count)
    return eng.snap(reg)


def postln_layer(nc, xT, x, wqkv, bqk, bv, wout, bout, w1T, b1, w2T, b2, out):
    ctx = ExitStack()
    with ctx:
        def sb(name, shape, dt=F32):
            return ctx.enter_context(nc.sbuf_tensor(name, shape, dt))

        def sem(name):
            return ctx.enter_context(nc.semaphore(name))

        WQKV = [sb("wqkv_hi", [P, KC, 3 * D], F32R), sb("wqkv_lo", [P, KC, 3 * D], F32R)]
        WOUT = [sb("wout_hi", [P, KC, D], F32R), sb("wout_lo", [P, KC, D], F32R)]
        W1Q = sb("w1q", [P, KC, FF], F32R)
        W2Q = sb("w2q", [P, FC, D], F32R)
        B1 = sb("b1_rows", [2, FF], F32R)
        ONES2 = sb("ones_rows", [2, S // 2], F32R)
        BQK = sb("bqk", [P, 4])
        BV = sb("bv_rep", [P, D])
        BOUT = sb("bout_rep", [P, D])
        B2 = sb("b2_rep", [P, D])
        IDN = sb("identity", [P, P])
        ONES = sb("ones", [P, P])
        BAND = sb("band", [P, 3 * W])
        XRAW = sb("x_raw", [P, KC, S])
        XT = [sb("xT_hi", [P, KC, S], F32R), sb("xT_lo", [P, KC, S], F32R)]
        QK = [[sb(f"qk{j}_hi", [P, S], F32R), sb(f"qk{j}_lo", [P, S], F32R)] for j in range(4)]
        SQ = sb("q_stack", [P, 8, S], F32R)
        SK = sb("k_stack", [P, 8, S], F32R)
        VN = sb("v_next", [P, TB, D])
        VAUG = sb("v_aug", [P, QUADS, TB, 4, 32])
        PR = sb("probs", [P, 2, 2, PW])
        U = sb("u", [P, S])
        RC = sb("recip", [P, TB * 4])
        ON = sb("o_norm", [P, TB, D])
        OT = [sb("oT_hi", [P, KC, S], F32R), sb("oT_lo", [P, KC, S], F32R)]
        Y = sb("y", [P, TB, D])
        X1 = sb("x1", [P, TB, D])
        X1T = [sb("x1T_hi", [P, KC, S], F32R), sb("x1T_lo", [P, KC, S], F32R)]
        HID = [sb("hid_hi", [P, FC, S // 2], F32R), sb("hid_lo", [P, FC, S // 2], F32R)]
        B1R = X1[0:1].rearrange("p t d -> p (t d)")
        RMAX = sb("rmax", [P, NB, 4])
        NM = sb("neg_max", [P, NB, 2, 4])
        NMT = sb("neg_maxT", [8, S], F32R)
        ST = sb("ln_stats", [P, TB, 6])
        MV1 = sb("ln1_mv", [P, TB, 2])
        MV2 = sb("ln2_mv", [P, TB, 2])
        VE = sb("var_eps", [P, TB])
        HALF = sb("minus_half", [P, TB])
        RS1 = sb("ln1_rstd", [P, TB])
        RS2 = sb("ln2_rstd", [P, TB])
        ABS = sb("abs_sums", [P, 2])
        THR = sb("thresholds", [P, 4])

        def bank(name):
            return ctx.enter_context(nc.psum_tensor(name, [P, 512], F32))

        PST = [bank("st_a"), bank("st_b"), bank("st_c")]
        PMX = [bank("mx_a"), bank("mx_b")]
        PUP = bank("pv")
        PG = [bank("gen_a"), bank("gen_b")]

        PRF = [PR[:, i].rearrange("p g w -> p (g w)") for i in range(2)]
        W1RAW = PRF[0][:, 0:KC * FF].rearrange("p (c n) -> p c n", c=KC)
        W2RAW = PRF[0][:, KC * FF:KC * FF + FC * D].rearrange("p (c n) -> p c n", c=FC)
        WQRAW = PRF[1][:, 0:KC * 3 * D].rearrange("p (c n) -> p c n", c=KC)
        WORAW = PRF[1][:, KC * 3 * D:KC * 4 * D].rearrange("p (c n) -> p c n", c=KC)
        QTMP = PRF[1][:, KC * 4 * D:KC * 4 * D + KC * FF].rearrange("p (c n) -> p c n", c=KC)

        s_wq = sem("wqkv_in")
        s_w12 = sem("w1_w2_in")
        s_small = sem("biases_in")
        s_const = sem("pool_constants")
        s_dconst = sem("dve_constants")
        s_abs = sem("abs_sums_done")
        s_gam = sem("abs_totals_full")
        s_thr = sem("thresholds_done")
        s_wsplit_h = sem("weights_hi")
        s_wsplit_l = sem("weights_lo")
        s_quant = sem("weights_quantised")
        s_x = sem("x_in")
        s_xh = sem("xT_hi_done")
        s_xl = sem("xT_lo_done")
        s_qkf = sem("qk_full")
        s_qkh = sem("qk_hi_done")
        s_qkl = sem("qk_lo_done")
        s_vf = sem("v_full")
        s_v = sem("v_next_done")
        s_va = sem("v_aug_done")
        s_stk = [sem(f"stack_in{v}") for v in range(4)]
        s_mxf = sem("max_scores_full")
        s_mxr = sem("max_read")
        s_nmh = sem("neg_max_hi")
        s_nm = sem("neg_max_done")
        s_nmtf = sem("neg_maxT_full")
        s_nmt = sem("neg_maxT_done")
        s_nmin = [sem(f"neg_max_in{v}") for v in range(4)]
        s_stf = sem("scores_full")
        s_exp = sem("exp_done")
        s_mask = sem("mask_done")
        s_pvf = sem("pv_full")
        s_u = sem("u_done")
        s_utf = sem("uT_full")
        s_rc = sem("recip_done")
        s_on = sem("o_norm_done")
        s_otf = sem("oT_full")
        s_oth = sem("oT_hi_done")
        s_otl = sem("oT_lo_done")
        s_xr = sem("x_residual_in")
        s_xrb = sem("x_residual_biased")
        s_opf = sem("out_proj_full")
        s_y = sem("y_done")
        s_st1 = sem("ln1_stats_done")
        s_mv1 = sem("ln1_mv_done")
        s_ve = sem("var_eps_done")
        s_rs1 = sem("ln1_rstd_done")
        s_x1 = sem("x1_done")
        s_x1tf = sem("x1T_full")
        s_x1h = sem("x1T_hi_done")
        s_x1l = sem("x1T_lo_done")
        s_x1b = sem("x1_biased")
        s_f1f = sem("ffn1_full")
        s_hh = sem("hidden_hi_done")
        s_hl = sem("hidden_lo_done")
        s_f2f = sem("ffn2_full")
        s_z = sem("z_done")
        s_st2 = sem("ln2_stats_done")
        s_mv2 = sem("ln2_mv_done")
        s_rs2 = sem("ln2_rstd_done")
        s_o = sem("out_done")
        s_od = sem("out_stored")

        block = ctx.enter_context(nc.Block())

        @block.sync
        def _(sp):
            sp.dma_start(WQRAW, wqkv.rearrange("(c p) n -> p c n", p=P)).then_inc(s_wq, 16)
            sp.dma_start(WORAW, wout.rearrange("(c p) n -> p c n", p=P)).then_inc(s_wq, 16)
            sp.dma_start(BQK[:, :], bqk).then_inc(s_small, 16)
            sp.dma_start(BV[:, :], bv[None, :].to_broadcast([P, D])).then_inc(s_small, 16)
            sp.dma_start(BOUT[:, :], bout[None, :].to_broadcast([P, D])).then_inc(s_small, 16)
            sp.dma_start(B2[:, :], b2[None, :].to_broadcast([P, D])).then_inc(s_small, 16)
            sp.dma_start(B1R, b1[None, :]).then_inc(s_small, 16)
            sp.dma_start(W1RAW, w1T.rearrange("(c p) n -> p c n", p=P)).then_inc(s_w12, 16)
            sp.dma_start(W2RAW, w2T.rearrange("(c p) n -> p c n", p=P)).then_inc(s_w12, 16)
            sp.wait_ge(s_wsplit_l, 3)
            sp.dma_start(B1[1:2, :].bitcast(F32), Y[0:1, :, :].rearrange("p t d -> p (t d)")).then_inc(s_small, 16)
            sp.wait_ge(s_small, 96)
            sp.wait_ge(s_const, POOL_CONSTANTS)

            def stack(r, v, first):
                c, ih = v // 2, v % 2
                sp.wait_ge(s_qkh, 4 * r + 2 * c + 2)
                sp.wait_ge(s_qkl, 4 * r + 2 * c + 2)
                if not first:
                    sp.wait_ge(s_stf, 12 * (4 * r - 4 + v) + 12)
                half = slice(64 * ih, 64 * ih + 64)
                heads = slice(4 * ih, 4 * ih + 4)
                for dst, j, terms in ((SQ, 2 * c, (0, 1, 0)), (SK, 2 * c + 1, (0, 0, 1))):
                    for t, part in enumerate(terms):
                        rows = slice(64 * c + 16 * t, 64 * c + 16 * t + 16)
                        sp.dma_start(dst[rows, heads, :].bitcast(F32), QK[j][part][half, :].bitcast(F32)).then_inc(s_stk[v], 16)

            def step(b, at):
                attn, post, nxt = stages(at)
                if nxt:
                    if at != -1:
                        sp.wait_ge(s_xh, b + 1)
                        sp.wait_ge(s_xl, b + 1)
                    sp.dma_start(XRAW[:, :, :], xT[bass.ds(b + 1, 1)].rearrange("a (c p) t -> p (a c) t", p=P)) \
                        .then_inc(s_x, 16)
                for v in range(4):
                    if v == 0 and post:
                        if at != 1:
                            sp.wait_ge(s_x1, 4 * (b - 1))
                        sp.dma_start(Y[:, :, :], x[bass.ds(b - 1, 1)].rearrange("a (t p) d -> p (a t) d", p=P)) \
                            .then_inc(s_xr, 16)
                    if v < 2 and attn:
                        stack(b, v + 2, at == 0)
                    if v >= 2 and nxt:
                        stack(b + 1, v - 2, at == -1)
                    q = max_quad(v, at)
                    if q is not None:
                        r, vq = b + q[0], q[1]
                        sp.wait_ge(s_nmt, 4 * r + vq + 1)
                        c, ih = vq // 2, vq % 2
                        sp.dma_start(SQ[64 * c + 48:64 * c + 50, 4 * ih:4 * ih + 4, :].bitcast(F32), NMT[:, :].bitcast(F32)) \
                            .then_inc(s_nmin[vq], 16)
                    if v >= 2 and post:
                        store(b, v - 2)

            def store(b, hf):
                sp.wait_ge(s_o, 4 * (b - 1) + 2 * hf + 2)
                sp.dma_start(out[bass.ds(b - 1, 1), 256 * hf:256 * hf + 256].rearrange("a (t p) d -> p (a t) d", p=P),
                             X1[:, 2 * hf:2 * hf + 2, :]).then_inc(s_od, 16)

            steps(sp, step)
            sp.wait_ge(s_od, 32 * B)

        @block.tensor
        def _(pe):
            pe.wait_ge(s_abs, 2)
            pe.wait_ge(s_dconst, 1)
            pe.matmul(PG[0][:, 0:2], ONES[:, :], ABS[:, :], start=True, stop=True).then_inc(s_gam, 1)
            pe.wait_ge(s_const, POOL_CONSTANTS)
            pe.wait_ge(s_wsplit_h, 3)
            pe.wait_ge(s_wsplit_l, 3)
            pe.wait_ge(s_thr, 1)

            reader = {0: None, 1: None}

            def bank_free(n, b):
                if reader[n] is not None:
                    s, per_row, count, dr = reader[n]
                    pe.wait_ge(s, per_row * (b + dr) + count)
                return PG[n]

            def scores(b, v, g, at):
                c, hd = v // 2, 4 * (v % 2) + g
                rows = slice(64 * c, 64 * c + 50)
                if g == 0:
                    pe.wait_ge(s_stk[v], 96 * b + 96)
                    pe.wait_ge(s_nmin[v], 16 * b + 16)
                for u, ms in enumerate(((1,), (2,), (3, 0))):
                    if not (at == 0 and v == 0 and g == 0):
                        pe.wait_ge(s_exp, 3 * (16 * b + 4 * v + g) - 2 + u)
                    at_col = 0
                    for m in ms:
                        _, _, q0, n = PCOL[m]
                        mm = pe.matmul(PST[u][:, at_col:at_col + n], SK[rows, hd, W * m:W * m + W],
                                       SQ[rows, hd, q0:q0 + n], start=True, stop=True)
                        at_col += n
                    mm.then_inc(s_stf, 1)

            def max_scores(r, v, i, first):
                g, n = i // 4, i % 4
                c, hd = v // 2, 4 * (v % 2) + g
                rows = slice(64 * c, 64 * c + 48)
                lo, hi = max(0, n - 1) * W, min(NB, n + 2) * W
                if i == 0:
                    pe.wait_ge(s_stk[v], 96 * r + 96)
                if not (first and i < 2):
                    pe.wait_ge(s_mxr, 16 * (4 * r + v) + i - 1)
                pe.matmul(PMX[i % 2][:, 0:hi - lo], SQ[rows, hd, W * n:W * n + W], SK[rows, hd, lo:hi],
                          start=True, stop=True).then_inc(s_mxf, 1)

            def split3(ps, lhs, rhs, last_inc=None):
                terms = [(a, z, kc) for kc in range(KC) for a, z in ((0, 0), (1, 0), (0, 1))]
                for n, (a, z, kc) in enumerate(terms):
                    mm = pe.matmul(ps, lhs(a, kc), rhs(z, kc), start=(n == 0), stop=(n == len(terms) - 1))
                return mm

            def side_work(v, step, b, dr, vq, at):
                name = name_of(step)
                r = b + dr
                first = at is not None and at + dr == 0
                G, n = None, BANK.get((v, step))
                if n is not None:
                    G = bank_free(n, b)
                if name == "pva" or name == "pvb":
                    q = 4 * r + vq
                    if name == "pva":
                        pe.wait_ge(s_mask, 2 * q + 2)
                        pe.wait_ge(s_va, q + 1)
                        if not (first and vq == 0):
                            pe.wait_ge(s_u, q)
                    for m in ((0, 1) if name == "pva" else (2, 3)):
                        col, pitch, q0, n = PCOL[m]
                        for g in range(4):
                            lo = col + pitch * (g % 2)
                            mm = pe.matmul(PUP[32 * g:32 * g + 32, q0:q0 + n], VAUG[:, vq, m, g, :],
                                           PR[:, vq % 2, g // 2, lo:lo + n], start=(m == 0), stop=(m == 3),
                                           skip_group_check=True)
                    if name == "pvb":
                        mm.then_inc(s_pvf, 1)
                elif name == "ut":
                    pe.wait_ge(s_u, 4 * r + vq + 1)
                    for t in range(TB):
                        mm = pe.transpose(G[:, P * t:P * t + P], U[:, P * t:P * t + P], IDN[:, :])
                    mm.then_inc(s_utf, 1)
                    reader[n] = (s_on, 4, vq + 1, dr)
                elif name == "nmt":
                    pe.wait_ge(s_nm, 4 * r + vq + 1)
                    for t in range(NB):
                        mm = pe.transpose(G[0:8, P * t:P * t + P], NM[:, t].rearrange("p a g -> p (a g)"), IDN[:, :])
                    mm.then_inc(s_nmtf, 1)
                    reader[n] = (s_nmt, 4, vq + 1, dr)
                elif name == "qk":
                    j = step[1]
                    if j == 0:
                        pe.wait_ge(s_xh, r + 1)
                        pe.wait_ge(s_xl, r + 1)
                    cols = slice(P * j, P * j + P)
                    split3(G[:, :], lambda a, kc: WQKV[a][:, kc, cols], lambda z, kc: XT[z][:, kc, :]) \
                        .then_inc(s_qkf, 1)
                    reader[n] = (s_qkl, 4, j + 1, dr)
                elif name == "vp":
                    i = step[1]
                    for t in (2 * i, 2 * i + 1):
                        mm = split3(G[:, D * (t % 2):D * (t % 2) + D],
                                    lambda a, kc: XT[a][:, kc, P * t:P * t + P],
                                    lambda z, kc: WQKV[z][:, kc, 2 * D:3 * D])
                    mm.then_inc(s_vf, 1)
                    reader[n] = (s_v, 2, i + 1, dr)
                elif name == "ot":
                    i = step[1]
                    pe.wait_ge(s_on, 4 * r + 4)
                    for t in range(TB):
                        mm = pe.transpose(G[:, P * t:P * t + P], ON[:, t, P * i:P * i + P], IDN[:, :])
                    mm.then_inc(s_otf, 1)
                    reader[n] = (s_otl, 2, i + 1, dr)
                elif name == "op":
                    i = step[1]
                    pe.wait_ge(s_oth, 2 * r + 2)
                    pe.wait_ge(s_otl, 2 * r + 2)
                    for t in (2 * i, 2 * i + 1):
                        mm = split3(G[:, D * (t % 2):D * (t % 2) + D],
                                    lambda a, kc: OT[a][:, kc, P * t:P * t + P],
                                    lambda z, kc: WOUT[z][:, kc, :])
                    mm.then_inc(s_opf, 1)
                    reader[n] = (s_y, 2, i + 1, dr)
                elif name == "x1t":
                    i = step[1]
                    pe.wait_ge(s_x1, 4 * r + 4)
                    for t in range(TB):
                        mm = pe.transpose(G[:, P * t:P * t + P], X1[:, t, P * i:P * i + P], IDN[:, :])
                    mm.then_inc(s_x1tf, 1)
                    reader[n] = (s_x1l, 2, i + 1, dr)
                elif name == "f1":
                    hf, p = step[1], step[2]
                    pe.wait_ge(s_x1h, 2 * r + 2)
                    pe.wait_ge(s_x1l, 2 * r + 2)
                    if first and hf == 0 and p == 0:
                        pe.wait_ge(s_quant, 2)
                        pe.wait_ge(s_small, 96)
                    for k, f in enumerate((2 * p, 2 * p + 1)):
                        ps = G[:, 256 * k:256 * k + 256]
                        pe.matmul(ps, B1[:, P * f:P * f + P], ONES2[:, :], start=True, stop=False)
                        for kc in range(KC):
                            for a in range(2):
                                mm = pe.matmul(ps, W1Q[:, kc, P * f:P * f + P],
                                               X1T[a][:, kc, 256 * hf:256 * hf + 256],
                                               start=False, stop=(kc == KC - 1 and a == 1))
                    mm.then_inc(s_f1f, 1)
                    reader[n] = (s_hl, 8, 4 * hf + p + 1, dr)
                elif name == "f2":
                    hf = step[1]
                    pe.wait_ge(s_hh, 8 * r + 4 * hf + 4)
                    pe.wait_ge(s_hl, 8 * r + 4 * hf + 4)
                    for t in range(2):
                        for f in range(FC):
                            for a in range(2):
                                mm = pe.matmul(G[:, D * t:D * t + D], HID[a][:, f, P * t:P * t + P],
                                               W2Q[:, f, :], start=(f == 0 and a == 0),
                                               stop=(f == FC - 1 and a == 1))
                    mm.then_inc(s_f2f, 1)
                    reader[n] = (s_z, 2, hf + 1, dr)

            def step(b, at):
                attn, _, _ = stages(at)
                for v in range(4):
                    q = max_quad(v, at)
                    for k in range(8):
                        if attn and k % 2 == 0:
                            scores(b, v, k // 2, at)
                        if q is not None:
                            for i in range(*MAXES[k]):
                                max_scores(b + q[0], q[1], i, at == -1)
                        for s, dr, vq in side(v, k, at):
                            side_work(v, s, b, dr, vq, at)
                for n in (0, 1):
                    if reader[n] is not None:
                        reader[n] = reader[n][:3] + (reader[n][3] - 1,)

            steps(pe, step)

        @block.scalar
        def _(act):
            act.wait_ge(s_w12, 32)
            act.wait_ge(s_dconst, 1)
            act.activation(HID[0][:, :, :], W1RAW.rearrange("p c (n f) -> p (c n) f", f=256), ACT.Abs,
                           accum_out=ABS[:, 0:1]).then_inc(s_abs, 1)
            act.activation(HID[1][:, :, :], W2RAW, ACT.Abs, accum_out=ABS[:, 1:2]).then_inc(s_abs, 1)
            act.wait_ge(s_wq, 32)
            act.wait_ge(s_small, 80)
            act.activation(WQKV[0][:, :, :], WQRAW, ACT.Identity).then_inc(s_wsplit_h, 1)
            act.activation(WOUT[0][:, :, :], WORAW, ACT.Identity).then_inc(s_wsplit_h, 1)
            act.activation(B1[0:1, :], B1R, ACT.Identity).then_inc(s_wsplit_h, 1)

            def exps(b, v, g, at):
                q = 4 * b + v
                if g == 0 and not (at == 0 and v < 2):
                    act.wait_ge(s_pvf, q - 1)
                if at == 0 and v == 0 and g == 0:
                    act.wait_ge(s_quant, 2)
                    act.wait_ge(s_wsplit_l, 3)
                for u, (first, n) in enumerate(((0, 384), (768, 384), (1536, 512))):
                    lo = first + n * (g % 2)
                    act.wait_ge(s_stf, 3 * (4 * q + g) + u + 1)
                    act.activation(PR[:, v % 2, g // 2, lo:lo + n], PST[u][:, 0:n], ACT.Exp, scale=SCALE) \
                        .then_inc(s_exp, 1)

            def side_work(v, step, b, dr, vq, at):
                name = name_of(step)
                r = b + dr
                first = at is not None and at + dr == 0
                n = BANK.get((v, step))
                G = PG[n] if n is not None else None
                if name == "xs":
                    act.wait_ge(s_x, 16 * r + 16)
                    if not first:
                        act.wait_ge(s_qkf, 4 * r)
                        act.wait_ge(s_vf, 2 * r)
                    act.activation(XT[0][:, :, :], XRAW[:, :, :], ACT.Identity).then_inc(s_xh, 1)
                elif name == "qk":
                    j = step[1]
                    act.wait_ge(s_qkf, 4 * r + j + 1)
                    if not first:
                        act.wait_ge(s_stk[2 * (j // 2)], 96 * r)
                        act.wait_ge(s_stk[2 * (j // 2) + 1], 96 * r)
                    act.activation(QK[j][0][:, :], G[:, :], ACT.Identity, bias=BQK[:, j:j + 1]) \
                        .then_inc(s_qkh, 1)
                elif name == "nmt":
                    q = 4 * r + vq
                    act.wait_ge(s_nmtf, q + 1)
                    if not (first and vq == 0):
                        act.wait_ge(s_nmin[(vq + 3) % 4], 16 * r + (0 if vq == 0 else 16))
                    act.activation(NMT[:, :], G[0:8, :], ACT.Identity).then_inc(s_nmt, 1)
                elif name == "pvb":
                    q = 4 * r + vq
                    act.wait_ge(s_pvf, q + 1)
                    if not (first and vq == 0):
                        act.wait_ge(s_utf, q)
                    act.activation(U[:, :], PUP[:, :], ACT.Identity).then_inc(s_u, 1)
                elif name == "ot":
                    i = step[1]
                    act.wait_ge(s_otf, 2 * r + i + 1)
                    if not first:
                        act.wait_ge(s_opf, 2 * r)
                    act.activation(OT[0][:, i, :], G[:, :], ACT.Identity).then_inc(s_oth, 1)
                elif name == "x1t":
                    i = step[1]
                    act.wait_ge(s_x1tf, 2 * r + i + 1)
                    if not first:
                        act.wait_ge(s_f1f, 8 * r)
                    act.activation(X1T[0][:, i, :], G[:, :], ACT.Identity).then_inc(s_x1h, 1)
                elif name == "f1":
                    hf, p = step[1], step[2]
                    act.wait_ge(s_f1f, 8 * r + 4 * hf + p + 1)
                    if not (first and hf == 0):
                        act.wait_ge(s_f2f, 2 * r + hf)
                    act.activation(HID[0][:, 2 * p:2 * p + 2, :].rearrange("p f t -> p (f t)"), G[:, :],
                                   ACT.Relu).then_inc(s_hh, 1)

            def step(b, at):
                attn, _, _ = stages(at)
                for v in range(4):
                    for k in range(8):
                        if attn and k % 2 == 0:
                            exps(b, v, k // 2, at)
                        for s, dr, vq in side(v, k, at):
                            side_work(v, s, b, dr, vq, at)

            steps(act, step)

        @block.vector
        def _(dve):
            dve.memset(ONES[:, :], 1.0).then_inc(s_dconst, 1)
            dve.wait_ge(s_gam, 1)
            dve.tensor_scalar(THR[:, 0:2], PG[0][:, 0:2], 1.0 / (D * FF), EPS, ALU.mult, ALU.add) \
                .then_inc(s_dconst, 1)
            dve.wait_ge(s_dconst, 2)
            dve.tensor_scalar(THR[:, 2:4], THR[:, 0:2], -0.5, None, ALU.mult).then_inc(s_dconst, 1)
            dve.wait_ge(s_dconst, 3)
            dve.tensor_scalar(THR[:, 0:2], THR[:, 0:2], 0.5, None, ALU.mult).then_inc(s_thr, 1)
            dve.wait_ge(s_wsplit_h, 3)
            dve.tensor_tensor(WQKV[1][:, :, :], WQRAW, WQKV[0][:, :, :].bitcast(F32), ALU.subtract) \
                .then_inc(s_wsplit_l, 1)
            dve.tensor_tensor(WOUT[1][:, :, :], WORAW, WOUT[0][:, :, :].bitcast(F32), ALU.subtract) \
                .then_inc(s_wsplit_l, 1)
            dve.tensor_tensor(Y[0:1, :, :].rearrange("p t d -> p (t d)"), B1R, B1[0:1, :].bitcast(F32),
                              ALU.subtract).then_inc(s_wsplit_l, 1)

            def quantise():
                dve.wait_ge(s_thr, 1)
                for i, (raw, dst) in enumerate(((W1RAW, W1Q), (W2RAW, W2Q))):
                    if i == 1:
                        dve.wait_ge(s_quant, 1)
                    tmp = QTMP if i == 0 else QTMP.rearrange("p c (n f) -> p (c n) f", f=D)
                    dve.tensor_scalar(tmp, raw, THR[:, 2 + i:3 + i], None, ALU.is_lt).then_inc(s_dconst, 1)
                    dve.wait_ge(s_dconst, 4 + i)
                    dve.scalar_tensor_tensor(dst[:, :, :], raw, THR[:, i:i + 1], tmp, ALU.is_gt, ALU.subtract) \
                        .then_inc(s_quant, 1)

            def row_max(r, v, i, first):
                g, n = i // 4, i % 4
                if i == 0 and not (first and v == 0):
                    count = in_register(dve, 4 * r + v)
                    dve.wait_ge(s_const, POOL_CONSTANTS)
                    dve.wait_ge(s_nm, count)
                a, z = (W if n == 0 else 0), (2 * W if n == NB - 1 else 3 * W)
                count = in_register(dve, 16 * (4 * r + v) + i + 1)
                dve.wait_ge(s_const, POOL_CONSTANTS)
                dve.wait_ge(s_mxf, count)
                ps = PMX[i % 2][:, 0:z - a]
                dve.tensor_tensor_reduce(ps, ps, BAND[:, a:z], 1.0, -3e38, ALU.add, ALU.max,
                                         RMAX[:, n, g:g + 1]).then_inc(s_mxr, 1)

            def neg_max(r, v, first):
                q = 4 * r + v
                dve.wait_ge(s_mxr, 16 * q + 16)
                if not (first and v == 0):
                    dve.wait_ge(s_nmtf, q)
                dve.tensor_scalar(NM[:, :, 0, :].bitcast(F32R), RMAX[:, :, :], -1.0, None, ALU.mult) \
                    .then_inc(s_nmh, 1)
                dve.wait_ge(s_nmh, q + 1)
                dve.scalar_tensor_tensor(NM[:, :, 1, :], RMAX[:, :, :], -1.0, NM[:, :, 0, :], ALU.mult,
                                         ALU.subtract).then_inc(s_nm, 1)

            def side_work(v, step, b, dr, vq, at):
                name = name_of(step)
                r = b + dr
                first = at is not None and at + dr == 0
                n = BANK.get((v, step))
                G = PG[n] if n is not None else None
                if name == "qk":
                    j = step[1]
                    dve.wait_ge(s_qkh, 4 * r + j + 1)
                    dve.scalar_tensor_tensor(QK[j][1][:, :], G[:, :], BQK[:, j:j + 1],
                                             QK[j][0][:, :].bitcast(F32), ALU.add, ALU.subtract) \
                        .then_inc(s_qkl, 1)
                elif name == "vp":
                    i = step[1]
                    dve.wait_ge(s_vf, 2 * r + i + 1)
                    if i == 0 and not first:
                        dve.wait_ge(s_va, 4 * r)
                    dve.tensor_tensor(VN[:, 2 * i:2 * i + 2, :], G[:, :].rearrange("p (t d) -> p t d", t=2),
                                      BV[:, None, :].to_broadcast([P, 2, D]), ALU.add).then_inc(s_v, 1)
                elif name == "ut":
                    q = 4 * r + vq
                    dve.wait_ge(s_utf, q + 1)
                    if not (first and vq == 0):
                        dve.wait_ge(s_on, q)
                    sums = G[:, :].rearrange("p (a e) -> p a e", e=32)
                    dve.reciprocal(RC[:, :], sums[:, :, 16]).then_inc(s_rc, 1)
                    dve.wait_ge(s_rc, q + 1)
                    if vq == 0 and not first:
                        dve.wait_ge(s_otf, 2 * r)
                    dve.tensor_tensor(ON[:, :, 64 * vq:64 * vq + 64].rearrange("p t (g d) -> p t g d", g=4),
                                      sums[:, :, 0:16].rearrange("p (t g) d -> p t g d", t=TB),
                                      RC[:, :].rearrange("p (t g) -> p t g", t=TB)[:, :, :, None]
                                      .to_broadcast([P, TB, 4, DH]), ALU.mult).then_inc(s_on, 1)
                elif name == "ot":
                    i = step[1]
                    dve.wait_ge(s_oth, 2 * r + i + 1)
                    dve.tensor_tensor(OT[1][:, i, :], G[:, :], OT[0][:, i, :].bitcast(F32), ALU.subtract) \
                        .then_inc(s_otl, 1)
                elif name == "op":
                    i = step[1]
                    dve.wait_ge(s_opf, 2 * r + i + 1)
                    dve.wait_ge(s_xrb, r + 1)
                    y = Y[:, 2 * i:2 * i + 2, :]
                    dve.tensor_tensor(y, G[:, :].rearrange("p (t d) -> p t d", t=2), y, ALU.add) \
                        .then_inc(s_y, 1)
                elif name == "ln1":
                    if not first:
                        dve.wait_ge(s_mv2, 4 * r)
                        dve.wait_ge(s_x1, 4 * r)
                    for t in range(TB):
                        dve.wait_ge(s_y, 2 * r + 1 + t // 2)
                        dve.bn_stats(ST[:, t, :], Y[:, t, :]).then_inc(s_st1, 1)
                    for t in range(TB):
                        count = in_register(dve, 4 * r + 1 + t)
                        dve.wait_ge(s_thr, 1)
                        dve.wait_ge(s_st1, count)
                        dve.bn_aggr(MV1[:, t, :], ST[:, t, :]).then_inc(s_mv1, 1)
                elif name == "x1":
                    dve.wait_ge(s_rs1, r + 1)
                    if not first:
                        dve.wait_ge(s_od, 32 * r)
                    for t in range(TB):
                        dve.tensor_scalar(X1[:, t, :], Y[:, t, :], MV1[:, t, 0:1], RS1[:, t:t + 1],
                                          ALU.subtract, ALU.mult).then_inc(s_x1, 1)
                elif name == "x1t":
                    i = step[1]
                    dve.wait_ge(s_x1h, 2 * r + i + 1)
                    dve.tensor_tensor(X1T[1][:, i, :], G[:, :], X1T[0][:, i, :].bitcast(F32), ALU.subtract) \
                        .then_inc(s_x1l, 1)
                elif name == "f1":
                    hf, p = step[1], step[2]
                    dve.wait_ge(s_hh, 8 * r + 4 * hf + p + 1)
                    pair = [h[:, 2 * p:2 * p + 2, :].rearrange("p f t -> p (f t)") for h in HID]
                    dve.scalar_tensor_tensor(pair[1], G[:, :], 0.0, pair[0].bitcast(F32), ALU.max,
                                             ALU.subtract).then_inc(s_hl, 1)
                elif name == "f2":
                    hf = step[1]
                    dve.wait_ge(s_f2f, 2 * r + hf + 1)
                    dve.wait_ge(s_x1b, r + 1)
                    z = X1[:, 2 * hf:2 * hf + 2, :]
                    dve.tensor_tensor(z, G[:, :].rearrange("p (t d) -> p t d", t=2), z, ALU.add) \
                        .then_inc(s_z, 1)
                elif name == "ln2":
                    hf = step[1]
                    dve.wait_ge(s_mv1, 4 * r + 4)
                    if not first:
                        dve.wait_ge(s_o, 4 * r)
                    dve.wait_ge(s_z, 2 * r + hf + 1)
                    for t in (2 * hf, 2 * hf + 1):
                        dve.bn_stats(ST[:, t, :], X1[:, t, :]).then_inc(s_st2, 1)
                    for t in (2 * hf, 2 * hf + 1):
                        count = in_register(dve, 4 * r + 1 + t)
                        dve.wait_ge(s_thr, 1)
                        dve.wait_ge(s_st2, count)
                        dve.bn_aggr(MV2[:, t, :], ST[:, t, :]).then_inc(s_mv2, 1)
                elif name == "out":
                    hf = step[1]
                    dve.wait_ge(s_rs2, 2 * r + hf + 1)
                    for t in (2 * hf, 2 * hf + 1):
                        dve.tensor_scalar(X1[:, t, :], X1[:, t, :], MV2[:, t, 0:1], RS2[:, t:t + 1],
                                          ALU.subtract, ALU.mult).then_inc(s_o, 1)

            def step(b, at):
                if at == 0:
                    quantise()
                for v in range(4):
                    q = max_quad(v, at)
                    for k in range(8):
                        if q is not None:
                            for i in range(*MAXES[k]):
                                row_max(b + q[0], q[1], i, at == -1)
                            if MAXES[k][0] < 16 == MAXES[k][1]:
                                neg_max(b + q[0], q[1], at == -1)
                        for s, dr, vq in side(v, k, at):
                            side_work(v, s, b, dr, vq, at)

            steps(dve, step)

        @block.gpsimd
        def _(pool):
            pool.memset(IDN[:, :], 0.0).then_inc(s_const, 1)
            pool.memset(BAND[:, :], 0.0).then_inc(s_const, 1)
            pool.wait_ge(s_const, 2)
            pool.affine_select(out=IDN[:, :], in_=IDN[:, :], compare_op=ALU.not_equal, fill=1.0, base=0,
                               pattern=[[-1, P]], channel_multiplier=1).then_inc(s_const, 1)
            pool.affine_select(out=BAND[:, 0:W], in_=BAND[:, 0:W], compare_op=ALU.is_ge, fill=MASKED, base=0,
                               pattern=[[1, W]], channel_multiplier=-1).then_inc(s_const, 1)
            pool.affine_select(out=BAND[:, 2 * W:3 * W], in_=BAND[:, 2 * W:3 * W], compare_op=ALU.is_ge,
                               fill=MASKED, base=0, pattern=[[-1, W]], channel_multiplier=1) \
                .then_inc(s_const, 1)

            pool.memset(HALF[:, :], -0.5).then_inc(s_const, 1)
            pool.memset(ONES2[:, :].bitcast(F32), 1.0).then_inc(s_const, 1)
            pool.memset(SK[:, :, :].bitcast(F32), 1.0).then_inc(s_const, 1)
            pool.memset(VAUG[:, :, :, :, :], 1.0).then_inc(s_const, 1)
            pool.wait_ge(s_const, POOL_CONSTANTS)

            def mask(b, v, g):
                count = in_register(pool, 3 * (16 * b + 4 * v + g) + 3)
                pool.wait_ge(s_const, POOL_CONSTANTS)
                pool.wait_ge(s_exp, count)
                pr = PR[:, v % 2, g // 2, :]
                inner = pr[:, 0:1536].rearrange("p (m w) -> p m w", w=384)
                outer = pr[:, 1536:2560].rearrange("p (h w) -> p h w", w=512)
                for pr_before, n in ((inner[:, :, 0:W], 4), (outer[:, :, 0:W], 2)):
                    pool.affine_select(out=pr_before, in_=pr_before, compare_op=ALU.is_ge, fill=0.0, base=0,
                                       pattern=[[0, n], [1, W]], channel_multiplier=-1)
                for pr_after, n in ((inner[:, :, 2 * W:3 * W], 4), (outer[:, :, 3 * W:4 * W], 2)):
                    last = pool.affine_select(out=pr_after, in_=pr_after, compare_op=ALU.is_ge, fill=0.0, base=0,
                                              pattern=[[0, n], [-1, W]], channel_multiplier=1)
                last.then_inc(s_mask, 1)

            def v_in_place(r, v, first):
                count = in_register(pool, 4 * (r - 1) + v + 1)
                made = in_register(pool, 2 * r + 2)
                pool.wait_ge(s_const, POOL_CONSTANTS)
                pool.wait_ge(s_v, made)
                if not first:
                    pool.wait_ge(s_pvf, count)
                pool.tensor_copy(VAUG[:, v, :, :, 0:DH],
                                 VN[:, :, 64 * v:64 * v + 64].rearrange("p t (g d) -> p t g d", g=4)) \
                    .then_inc(s_va, 1)

            def side_work(v, step, b, dr, vq, at):
                name = name_of(step)
                r = b + dr
                if name == "xs":
                    pool.wait_ge(s_xh, r + 1)
                    pool.tensor_tensor(XT[1][:, :, :], XRAW[:, :, :], XT[0][:, :, :].bitcast(F32),
                                       ALU.subtract).then_inc(s_xl, 1)
                elif name == "ot" and step[1] == 0:
                    pool.wait_ge(s_xr, 16 * r + 16)
                    pool.tensor_tensor(Y[:, :, :], Y[:, :, :], BOUT[:, None, :].to_broadcast([P, TB, D]),
                                       ALU.add).then_inc(s_xrb, 1)
                elif name == "ln1":
                    count = in_register(pool, 4 * r + 4)
                    pool.wait_ge(s_const, POOL_CONSTANTS)
                    pool.wait_ge(s_mv1, count)
                    pool.tensor_scalar(VE[:, :], MV1[:, :, 1], 1.0, EPS, ALU.mult, ALU.add).then_inc(s_ve, 1)
                    pool.wait_ge(s_ve, 3 * r + 1)
                    pool.tensor_tensor(RS1[:, :], VE[:, :], HALF[:, :], ALU.pow).then_inc(s_rs1, 1)
                elif name == "x1t" and step[1] == 1:
                    pool.wait_ge(s_x1tf, 2 * r + 2)
                    pool.tensor_tensor(X1[:, :, :], X1[:, :, :], B2[:, None, :].to_broadcast([P, TB, D]),
                                       ALU.add).then_inc(s_x1b, 1)
                elif name == "ln2":
                    hf = step[1]
                    two = slice(2 * hf, 2 * hf + 2)
                    count = in_register(pool, 4 * r + 2 * hf + 2)
                    pool.wait_ge(s_const, POOL_CONSTANTS)
                    pool.wait_ge(s_mv2, count)
                    pool.tensor_scalar(VE[:, two], MV2[:, two, 1], 1.0, EPS, ALU.mult, ALU.add).then_inc(s_ve, 1)
                    pool.wait_ge(s_ve, 3 * r + 2 + hf)
                    pool.tensor_tensor(RS2[:, two], VE[:, two], HALF[:, two], ALU.pow).then_inc(s_rs2, 1)

            def step(b, at):
                attn, _, _ = stages(at)
                for v in range(4):
                    for k in range(8):
                        if attn and k in (3, 7):
                            mask(b, v, k // 2)
                        if v == 0 and k == 0 and attn:
                            for vq in range(3):
                                v_in_place(b, vq, at == 0)
                        if v == 0 and k == 5 and attn:
                            v_in_place(b, 3, at == 0)
                        for s, dr, vq in side(v, k, at):
                            side_work(v, s, b, dr, vq, at)

            steps(pool, step)


def kernel(L0_attn_x, L0_attn_Wqkv, L0_attn_bqkv, L0_attn_Wout, L0_attn_bout, L0_ffn_W1, L0_ffn_b1,
           L0_ffn_W2, L0_ffn_b2):
    import numpy as np
    from concourse import bacc
    from concourse.bass_utils import run_bass_kernel_spmd

    x = np.ascontiguousarray(L0_attn_x)
    wqkv = np.asarray(L0_attn_Wqkv)
    bqkv = np.asarray(L0_attn_bqkv)
    order = np.arange(2 * D).reshape(2, 2, 2, 4, DH).transpose(1, 0, 2, 4, 3).reshape(-1)
    arrays = {
        "x": x,
        "xT": np.ascontiguousarray(x.transpose(0, 2, 1)),
        "wqkv": np.ascontiguousarray(np.concatenate([wqkv[:, order], wqkv[:, 2 * D:]], axis=1)),
        "bqk": np.ascontiguousarray(bqkv[order].reshape(4, P).T),
        "bv": np.ascontiguousarray(bqkv[2 * D:]),
        "wout": np.ascontiguousarray(L0_attn_Wout),
        "bout": np.ascontiguousarray(L0_attn_bout),
        "w1T": np.ascontiguousarray(np.asarray(L0_ffn_W1).T),
        "b1": np.ascontiguousarray(L0_ffn_b1),
        "w2T": np.ascontiguousarray(np.asarray(L0_ffn_W2).T),
        "b2": np.ascontiguousarray(L0_ffn_b2),
    }
    nc = bacc.Bacc("TRN2", target_bir_lowering=False, num_devices=1)
    aps = {n: nc.dram_tensor(f"in_{n}", a.shape, mybir.dt.from_np(a.dtype), kind="ExternalInput").ap()
           for n, a in arrays.items()}
    out = nc.dram_tensor("out", (B, S, D), F32, kind="ExternalOutput").ap()
    postln_layer(nc, out=out, **aps)
    result = run_bass_kernel_spmd(nc, [{f"in_{n}": a for n, a in arrays.items()}], core_ids=[0])
    return result.results[0]["out"]
```

```python
from contextlib import ExitStack

import concourse.bass as bass
from concourse import mybir

F32 = mybir.dt.float32
F32R = mybir.dt.float32r
BF16 = mybir.dt.bfloat16
ALU = mybir.AluOpType
ACT = mybir.ActivationFunctionType

P = 128
B, S, D = 16, 512, 256
H, DH, W = 16, 16, 128
FF = 1024
NB = S // W
KC = D // P
FC = FF // P
QUADS = H // 4
TB = S // P
EPS = 1e-5
SCALE = 1.0 / 16.0
MASKED = -1e30
POOL_CONSTANTS = 9

PCOL = {1: (0, 384, 0, 384), 2: (768, 384, 128, 384), 3: (1536, 512, 256, 256), 0: (1792, 512, 0, 256)}
PW = 2560

SIDE = [
    [("qk", 0), "nmt", "pva", "pvb", ("qk", 1), "ut", ("vp", 0), ("ot", 0), ("ot", 1), ("qk", 2), ("op", 0), ("op", 1),
     "ln1"],
    [("vp", 1), "nmt", ("qk", 3), "pva", "pvb", ("x1t", 0), ("x1t", 1), "ut", ("f1", 0, 0), ("f1", 0, 1)],
    [("f1", 0, 2), "xs", "nmt", ("f1", 0, 3), "pva", "pvb", ("f2", 0), "ut", ("f1", 1, 0), ("ln2", 0)],
    [("f1", 1, 1), "nmt", ("f1", 1, 2), "pva", ("f1", 1, 3), "pvb", "ut", ("f2", 1), ("ln2", 1)],
]
COST = {"qk": (3072, 6), "vp": (3072, 12), "op": (3072, 12), "ut": (1024, 4), "ot": (1024, 4), "x1t": (1024, 4),
        "nmt": (800, 4), "f1": (2560, 10), "f2": (8192, 32), "pva": (3200, 2), "pvb": (3200, 2)}
SCORE_UNITS, MAX_UNITS = 12, 16
LAG = {"qk": 1, "ot": 1, "x1t": 1, "f1": 1, "op": 1, "ut": 1, "f2": 1}
N_SHARED = 3

USES_BANK = {"ut", "qk", "ot", "op", "vp", "x1t", "f1", "f2", "nmt"}
POST = {"ot", "op", "ln1", "x1t", "f1", "f2", "ln2"}


def name_of(step):
    return step if isinstance(step, str) else step[0]


def banks():
    out, n = {}, 0
    for v in range(QUADS):
        for step in SIDE[v]:
            if name_of(step) in USES_BANK:
                out[(v, step)] = n % N_SHARED
                n += 1
    assert n % N_SHARED == 0
    return out


NEEDS = {"ot": "ut", "op": "ot", "f1": "x1t", "f2": "f1"}


def weave():
    out = []
    for v in range(QUADS):
        total = sum(COST.get(name_of(s), (0, 0))[0] for s in SIDE[v])
        units = [((i + 0.2) / SCORE_UNITS * total * 0.93, "scores", i) for i in range(SCORE_UNITS)]
        units += [((i + 0.3) / MAX_UNITS * total, "max", i) for i in range(MAX_UNITS)]
        units.sort()
        at, slot = 0, []
        for s in SIDE[v]:
            cost, places = COST.get(name_of(s), (0, 0))
            slot.append([(int((pos - at) / cost * places), kind, i)
                         for pos, kind, i in units if cost and at <= pos < at + cost])
            at += cost
        out.append(slot)
    return out


BANK = banks()
WOVEN = weave()


def stages(at):
    if at is None:
        return True, True, True, True
    return 0 <= at < B, 1 <= at <= B, 0 <= at + 1 < B, 0 <= at + 2 < B


def row_of(v, step, at):
    attn, post, nxt, nxt2 = stages(at)
    name = name_of(step)
    if name in POST:
        return (-1, None) if post else None
    if name in ("qk", "vp"):
        return (1, None) if nxt else None
    if name == "xs":
        return (2, None) if nxt2 else None
    if name == "nmt":
        if v < 3:
            return (0, v + 1) if attn else None
        return (1, 0) if nxt else None
    if v == 0:
        return (-1, 3) if post else None
    return (0, v - 1) if attn else None


def max_quad(v, at):
    attn, _, nxt, _ = stages(at)
    if v < 2:
        return (0, v + 2) if attn else None
    return (1, v - 2) if nxt else None


def dve_order(v):
    out, late, maxima = [], [], 0

    def due(now):
        while late and late[0][0] <= now:
            out.append(("side", late.pop(0)[1]))

    for step, woven in zip(SIDE[v], WOVEN[v]):
        while late and (any(name_of(s) == NEEDS.get(name_of(step)) for _, s in late)
                        or name_of(step) in USES_BANK and len(late) >= N_SHARED):
            out.append(("side", late.pop(0)[1]))
        for _, kind, i in woven:
            if kind == "max":
                out.append(("max", i))
                maxima += 1
                due(maxima)
        late.append((maxima + LAG.get(name_of(step), 0), step))
        due(maxima)
    due(MAX_UNITS + 100)
    return out


def steps(eng, step):
    for at in (-2, -1, 0):
        step(at, at)
    with eng.Fori(1, B - 2) as b:
        step(b, None)
    for at in (B - 2, B - 1, B):
        step(at, at)


def in_register(eng, count):
    if isinstance(count, int):
        return count
    reg = eng.alloc_register()
    eng.reg_mov(reg, count)
    return eng.snap(reg)


def postln_layer(nc, xT, x, wqkv, bqk, bv, wout, bout, w1T, b1, w2T, b2, out):
    ctx = ExitStack()
    with ctx:
        def sb(name, shape, dt=F32):
            return ctx.enter_context(nc.sbuf_tensor(name, shape, dt))

        def sem(name):
            return ctx.enter_context(nc.semaphore(name))

        WQKV = [sb("wqkv_hi", [P, KC, 3 * D], F32R), sb("wqkv_lo", [P, KC, 3 * D], F32R)]
        WOUT = [sb("wout_hi", [P, KC, D], F32R), sb("wout_lo", [P, KC, D], F32R)]
        W1Q = sb("w1q", [P, KC, FF], F32R)
        W2Q = sb("w2q", [P, FC, D], F32R)
        B1 = sb("b1_rows", [2, FF], F32R)
        ONES2 = sb("ones_rows", [2, S // 2], F32R)
        BQK = sb("bqk", [P, 4])
        BV = sb("bv_cols", [P, KC])
        BOUT = sb("bout_rep", [P, D])
        B2 = sb("b2_rep", [P, D])
        IDN = sb("identity", [P, P])
        ONES = sb("ones", [P, P])
        BAND = sb("band", [P, 3 * W])
        XRAW = sb("x_raw", [P, KC, S])
        XT = [sb("xT_hi", [P, KC, S], F32R), sb("xT_lo", [P, KC, S], F32R)]
        QK = [[sb(f"qk{j}_hi", [P, S], F32R), sb(f"qk{j}_lo", [P, S], F32R)] for j in range(4)]
        SQ = sb("q_stack", [P, 8, S], F32R)
        SK = sb("k_stack", [P, 8, S], F32R)
        VN = sb("v_next", [P, TB, D])
        VAUG = sb("v_aug", [P, QUADS, TB, 4, 32])
        PR = sb("probs", [P, 2, 2, PW])
        U = sb("u", [P, S])
        RC = sb("recip", [P, TB * 4])
        ON = sb("o_norm", [P, TB, D])
        OT = [sb("oT_hi", [P, KC, S], F32R), sb("oT_lo", [P, KC, S], F32R)]
        Y = sb("y", [P, TB, D])
        X1 = sb("x1", [P, TB, D])
        X1T = [sb("x1T_hi", [P, KC, S], F32R), sb("x1T_lo", [P, KC, S], F32R)]
        HID = [sb("hid_hi", [P, FC, S // 2], F32R), sb("hid_lo", [P, FC, S // 2], F32R)]
        B1R = X1[0:1].rearrange("p t d -> p (t d)")
        RMAX = sb("rmax", [P, NB, 4])
        NM = sb("neg_max", [P, NB, 2, 4])
        NMT = sb("neg_maxT", [8, S], F32R)
        ST = sb("ln_stats", [P, TB, 6])
        MV1 = sb("ln1_mv", [P, TB, 2])
        MV2 = sb("ln2_mv", [P, TB, 2])
        VE = sb("var_eps", [P, TB])
        HALF = sb("minus_half", [P, TB])
        RS1 = sb("ln1_rstd", [P, TB])
        RS2 = sb("ln2_rstd", [P, TB])
        ABS = sb("abs_sums", [P, 2])
        THR = sb("thresholds", [P, 4])

        def bank(name):
            return ctx.enter_context(nc.psum_tensor(name, [P, 512], F32))

        PST = [bank("st_a"), bank("st_b")]
        PMX = [bank("mx_a"), bank("mx_b")]
        PUP = bank("pv")
        PG = [bank(f"shared{n}") for n in range(N_SHARED)]

        PRF = [PR[:, i].rearrange("p g w -> p (g w)") for i in range(2)]
        W1RAW = PRF[0][:, 0:KC * FF].rearrange("p (c n) -> p c n", c=KC)
        W2RAW = PRF[0][:, KC * FF:KC * FF + FC * D].rearrange("p (c n) -> p c n", c=FC)
        WQRAW = PRF[1][:, 0:KC * 3 * D].rearrange("p (c n) -> p c n", c=KC)
        WORAW = PRF[1][:, KC * 3 * D:KC * 4 * D].rearrange("p (c n) -> p c n", c=KC)
        QTMP = PRF[1][:, KC * 4 * D:KC * 4 * D + KC * FF].rearrange("p (c n) -> p c n", c=KC)

        s_wq = sem("wqkv_in")
        s_w12 = sem("w1_w2_in")
        s_small = sem("biases_in")
        s_const = sem("pool_constants")
        s_dconst = sem("dve_constants")
        s_abs = sem("abs_sums_done")
        s_gam = sem("abs_totals_full")
        s_thr = sem("thresholds_done")
        s_wsplit_h = sem("weights_hi")
        s_wsplit_l = sem("weights_lo")
        s_quant = sem("weights_quantised")
        s_x = sem("x_in")
        s_xh = sem("xT_hi_done")
        s_xl = sem("xT_lo_done")
        s_qkf = sem("qk_full")
        s_qkh = sem("qk_hi_done")
        s_qkl = sem("qk_lo_done")
        s_vf = sem("v_full")
        s_v = sem("v_next_done")
        s_va = sem("v_aug_done")
        s_stk = [sem(f"stack_in{v}") for v in range(4)]
        s_mxf = sem("max_scores_full")
        s_mxr = sem("max_read")
        s_nmh = sem("neg_max_hi")
        s_nm = sem("neg_max_done")
        s_nmtf = sem("neg_maxT_full")
        s_nmt = sem("neg_maxT_done")
        s_nmin = [sem(f"neg_max_in{v}") for v in range(4)]
        s_stf = sem("scores_full")
        s_exp = sem("exp_done")
        s_mask = sem("mask_done")
        s_pvf = sem("pv_full")
        s_u = sem("u_done")
        s_utf = sem("uT_full")
        s_rc = sem("recip_done")
        s_on = sem("o_norm_done")
        s_otf = sem("oT_full")
        s_oth = sem("oT_hi_done")
        s_otl = sem("oT_lo_done")
        s_xr = sem("x_residual_in")
        s_xrb = sem("x_residual_biased")
        s_opf = sem("out_proj_full")
        s_y = sem("y_done")
        s_st1 = sem("ln1_stats_done")
        s_mv1 = sem("ln1_mv_done")
        s_ve = sem("var_eps_done")
        s_rs1 = sem("ln1_rstd_done")
        s_x1 = sem("x1_done")
        s_x1tf = sem("x1T_full")
        s_x1h = sem("x1T_hi_done")
        s_x1l = sem("x1T_lo_done")
        s_x1b = sem("x1_biased")
        s_f1f = sem("ffn1_full")
        s_hh = sem("hidden_hi_done")
        s_hl = sem("hidden_lo_done")
        s_f2f = sem("ffn2_full")
        s_z = sem("z_done")
        s_st2 = sem("ln2_stats_done")
        s_mv2 = sem("ln2_mv_done")
        s_rs2 = sem("ln2_rstd_done")
        s_o = sem("out_done")
        s_od = sem("out_stored")

        block = ctx.enter_context(nc.Block())

        @block.sync
        def _(sp):
            sp.dma_start(WQRAW, wqkv.rearrange("(c p) n -> p c n", p=P)).then_inc(s_wq, 16)
            sp.dma_start(WORAW, wout.rearrange("(c p) n -> p c n", p=P)).then_inc(s_wq, 16)
            sp.dma_start(BQK[:, :], bqk).then_inc(s_small, 16)
            sp.dma_start(BV[:, :], bv).then_inc(s_small, 16)
            sp.dma_start(BOUT[:, :], bout[None, :].to_broadcast([P, D])).then_inc(s_small, 16)
            sp.dma_start(B2[:, :], b2[None, :].to_broadcast([P, D])).then_inc(s_small, 16)
            sp.dma_start(B1R, b1[None, :]).then_inc(s_small, 16)
            sp.dma_start(W1RAW, w1T.rearrange("(c p) n -> p c n", p=P)).then_inc(s_w12, 16)
            sp.dma_start(W2RAW, w2T.rearrange("(c p) n -> p c n", p=P)).then_inc(s_w12, 16)
            sp.wait_ge(s_wsplit_l, 3)
            sp.dma_start(B1[1:2, :].bitcast(F32), Y[0:1, :, :].rearrange("p t d -> p (t d)")).then_inc(s_small, 16)
            sp.wait_ge(s_small, 96)
            sp.wait_ge(s_const, POOL_CONSTANTS)

            def stack(r, v, first):
                c, ih = v // 2, v % 2
                sp.wait_ge(s_qkh, 4 * r + 2 * c + 2)
                sp.wait_ge(s_qkl, 4 * r + 2 * c + 2)
                if not first:
                    sp.wait_ge(s_stf, 12 * (4 * r - 4 + v) + 12)
                half = slice(64 * ih, 64 * ih + 64)
                heads = slice(4 * ih, 4 * ih + 4)
                for dst, j, terms in ((SQ, 2 * c, (0, 1, 0)), (SK, 2 * c + 1, (0, 0, 1))):
                    for t, part in enumerate(terms):
                        rows = slice(64 * c + 16 * t, 64 * c + 16 * t + 16)
                        sp.dma_start(dst[rows, heads, :].bitcast(F32), QK[j][part][half, :].bitcast(F32)).then_inc(s_stk[v], 16)

            def step(b, at):
                attn, post, nxt, nxt2 = stages(at)
                if nxt2:
                    if at != -2:
                        sp.wait_ge(s_xh, b + 2)
                        sp.wait_ge(s_xl, b + 2)
                    sp.dma_start(XRAW[:, :, :], xT[bass.ds(b + 2, 1)].rearrange("a (c p) t -> p (a c) t", p=P)) \
                        .then_inc(s_x, 16)
                for v in range(QUADS):
                    if v == 0 and attn:
                        stack(b, 3, at == 0)
                    if v > 0 and nxt:
                        stack(b + 1, v - 1, at == -1)
                    if v == 0 and post:
                        if at != 1:
                            sp.wait_ge(s_x1, 4 * (b - 1))
                        sp.dma_start(Y[:, :, :], x[bass.ds(b - 1, 1)].rearrange("a (t p) d -> p (a t) d", p=P)) \
                            .then_inc(s_xr, 16)
                    q = row_of(v, "nmt", at)
                    if q is not None:
                        r, vq = b + q[0], q[1]
                        sp.wait_ge(s_nmt, 4 * r + vq + 1)
                        c, ih = vq // 2, vq % 2
                        sp.dma_start(SQ[64 * c + 48:64 * c + 50, 4 * ih:4 * ih + 4, :].bitcast(F32),
                                     NMT[:, :].bitcast(F32)).then_inc(s_nmin[vq], 16)
                if post:
                    store(b, 0)
                    store(b, 1)

            def store(b, hf):
                sp.wait_ge(s_o, 4 * (b - 1) + 2 * hf + 2)
                sp.dma_start(out[bass.ds(b - 1, 1), 256 * hf:256 * hf + 256].rearrange("a (t p) d -> p (a t) d", p=P),
                             X1[:, 2 * hf:2 * hf + 2, :]).then_inc(s_od, 16)

            steps(sp, step)
            sp.wait_ge(s_od, 32 * B)

        @block.tensor
        def _(pe):
            pe.wait_ge(s_abs, 2)
            pe.wait_ge(s_dconst, 1)
            pe.matmul(PG[0][:, 0:2], ONES[:, :], ABS[:, :], start=True, stop=True).then_inc(s_gam, 1)
            pe.wait_ge(s_const, POOL_CONSTANTS)
            pe.wait_ge(s_wsplit_h, 3)
            pe.wait_ge(s_wsplit_l, 3)
            pe.wait_ge(s_thr, 1)

            reader = [None] * N_SHARED

            def bank_free(n, b):
                if reader[n] is not None:
                    s, per_row, count, dr = reader[n]
                    pe.wait_ge(s, per_row * (b + dr) + count)
                return PG[n]

            def scores(b, v, i, at):
                g, u = i // 3, i % 3
                c, hd = v // 2, 4 * (v % 2) + g
                rows = slice(64 * c, 64 * c + 50)
                if i == 0:
                    pe.wait_ge(s_stk[v], 96 * b + 96)
                    pe.wait_ge(s_nmin[v], 16 * b + 16)
                if not (at == 0 and v == 0 and i < 2):
                    pe.wait_ge(s_exp, 12 * (4 * b + v) + i - 1)
                col = 0
                for m in ((1,), (2,), (3, 0))[u]:
                    _, _, q0, n = PCOL[m]
                    mm = pe.matmul(PST[i % 2][:, col:col + n], SK[rows, hd, W * m:W * m + W],
                                   SQ[rows, hd, q0:q0 + n], start=True, stop=True)
                    col += n
                mm.then_inc(s_stf, 1)

            def max_scores(r, v, i, first):
                g, n = i // 4, i % 4
                c, hd = v // 2, 4 * (v % 2) + g
                rows = slice(64 * c, 64 * c + 48)
                lo, hi = max(0, n - 1) * W, min(NB, n + 2) * W
                if i == 0:
                    pe.wait_ge(s_stk[v], 96 * r + 96)
                if not (first and v == 0 and i < 2):
                    pe.wait_ge(s_mxr, 16 * (4 * r + v) + i - 1)
                pe.matmul(PMX[i % 2][:, 0:hi - lo], SQ[rows, hd, W * n:W * n + W], SK[rows, hd, lo:hi],
                          start=True, stop=True).then_inc(s_mxf, 1)

            def split3(ps, lhs, rhs, passed):
                terms = [(a, z, kc) for kc in range(KC) for a, z in ((0, 0), (1, 0), (0, 1))]
                for n, (a, z, kc) in enumerate(terms):
                    passed()
                    mm = pe.matmul(ps, lhs(a, kc), rhs(z, kc), start=(n == 0), stop=(n == len(terms) - 1))
                return mm

            def side_work(v, step, b, dr, vq, at, passed):
                name = name_of(step)
                r = b + dr
                first = at is not None and at + dr == 0
                G, n = None, BANK.get((v, step))
                if n is not None:
                    G = bank_free(n, b)
                if name == "pva" or name == "pvb":
                    q = 4 * r + vq
                    if name == "pva":
                        pe.wait_ge(s_mask, 2 * q + 2)
                        pe.wait_ge(s_va, q + 1)
                        if not (first and vq == 0):
                            pe.wait_ge(s_u, q)
                    for m in ((0, 1) if name == "pva" else (2, 3)):
                        passed()
                        col, pitch, q0, n = PCOL[m]
                        for g in range(4):
                            lo = col + pitch * (g % 2)
                            mm = pe.matmul(PUP[32 * g:32 * g + 32, q0:q0 + n], VAUG[:, vq, m, g, :],
                                           PR[:, vq % 2, g // 2, lo:lo + n], start=(m == 0), stop=(m == 3),
                                           skip_group_check=True)
                    if name == "pvb":
                        mm.then_inc(s_pvf, 1)
                elif name == "ut":
                    pe.wait_ge(s_u, 4 * r + vq + 1)
                    for t in range(TB):
                        passed()
                        mm = pe.transpose(G[:, P * t:P * t + P], U[:, P * t:P * t + P], IDN[:, :])
                    mm.then_inc(s_utf, 1)
                    reader[n] = (s_on, 4, vq + 1, dr)
                elif name == "nmt":
                    pe.wait_ge(s_nm, 4 * r + vq + 1)
                    for t in range(NB):
                        passed()
                        mm = pe.transpose(G[0:8, P * t:P * t + P], NM[:, t].rearrange("p a g -> p (a g)"), IDN[:, :])
                    mm.then_inc(s_nmtf, 1)
                    reader[n] = (s_nmt, 4, vq + 1, dr)
                elif name == "qk":
                    j = step[1]
                    if j == 0:
                        pe.wait_ge(s_xh, r + 1)
                        pe.wait_ge(s_xl, r + 1)
                    cols = slice(P * j, P * j + P)
                    split3(G[:, :], lambda a, kc: WQKV[a][:, kc, cols], lambda z, kc: XT[z][:, kc, :], passed) \
                        .then_inc(s_qkf, 1)
                    reader[n] = (s_qkl, 4, j + 1, dr)
                elif name == "vp":
                    i = step[1]
                    for t in (2 * i, 2 * i + 1):
                        mm = split3(G[:, D * (t % 2):D * (t % 2) + D],
                                    lambda a, kc: XT[a][:, kc, P * t:P * t + P],
                                    lambda z, kc: WQKV[z][:, kc, 2 * D:3 * D], passed)
                    mm.then_inc(s_vf, 1)
                    reader[n] = (s_v, 2, i + 1, dr)
                elif name == "ot":
                    i = step[1]
                    pe.wait_ge(s_on, 4 * r + 4)
                    for t in range(TB):
                        passed()
                        mm = pe.transpose(G[:, P * t:P * t + P], ON[:, t, P * i:P * i + P], IDN[:, :])
                    mm.then_inc(s_otf, 1)
                    reader[n] = (s_otl, 2, i + 1, dr)
                elif name == "op":
                    i = step[1]
                    pe.wait_ge(s_oth, 2 * r + 2)
                    pe.wait_ge(s_otl, 2 * r + 2)
                    for t in (2 * i, 2 * i + 1):
                        mm = split3(G[:, D * (t % 2):D * (t % 2) + D],
                                    lambda a, kc: OT[a][:, kc, P * t:P * t + P],
                                    lambda z, kc: WOUT[z][:, kc, :], passed)
                    mm.then_inc(s_opf, 1)
                    reader[n] = (s_y, 2, i + 1, dr)
                elif name == "x1t":
                    i = step[1]
                    pe.wait_ge(s_x1, 4 * r + 4)
                    for t in range(TB):
                        passed()
                        mm = pe.transpose(G[:, P * t:P * t + P], X1[:, t, P * i:P * i + P], IDN[:, :])
                    mm.then_inc(s_x1tf, 1)
                    reader[n] = (s_x1l, 2, i + 1, dr)
                elif name == "f1":
                    hf, p = step[1], step[2]
                    pe.wait_ge(s_x1h, 2 * r + 2)
                    pe.wait_ge(s_x1l, 2 * r + 2)
                    if first and hf == 0 and p == 0:
                        pe.wait_ge(s_quant, 2)
                        pe.wait_ge(s_small, 96)
                    for k, f in enumerate((2 * p, 2 * p + 1)):
                        ps = G[:, 256 * k:256 * k + 256]
                        passed()
                        pe.matmul(ps, B1[:, P * f:P * f + P], ONES2[:, :], start=True, stop=False)
                        for kc in range(KC):
                            for a in range(2):
                                passed()
                                mm = pe.matmul(ps, W1Q[:, kc, P * f:P * f + P],
                                               X1T[a][:, kc, 256 * hf:256 * hf + 256],
                                               start=False, stop=(kc == KC - 1 and a == 1))
                    mm.then_inc(s_f1f, 1)
                    reader[n] = (s_hl, 8, 4 * hf + p + 1, dr)
                elif name == "f2":
                    hf = step[1]
                    pe.wait_ge(s_hh, 8 * r + 4 * hf + 4)
                    pe.wait_ge(s_hl, 8 * r + 4 * hf + 4)
                    for t in range(2):
                        for f in range(FC):
                            for a in range(2):
                                passed()
                                mm = pe.matmul(G[:, D * t:D * t + D], HID[a][:, f, P * t:P * t + P],
                                               W2Q[:, f, :], start=(f == 0 and a == 0),
                                               stop=(f == FC - 1 and a == 1))
                    mm.then_inc(s_f2f, 1)
                    reader[n] = (s_z, 2, hf + 1, dr)

            def step(b, at):
                attn = stages(at)[0]
                for v in range(QUADS):
                    q = max_quad(v, at)
                    for step, woven in zip(SIDE[v], WOVEN[v]):
                        places = [0]

                        def units(until):
                            for place, kind, i in woven:
                                if places[0] <= place < until:
                                    if kind == "scores" and attn:
                                        scores(b, v, i, at)
                                    elif kind == "max" and q is not None:
                                        max_scores(b + q[0], q[1], i, at == -1)
                            places[0] = until

                        def passed():
                            units(places[0] + 1)

                        row = row_of(v, step, at)
                        if row is not None and name_of(step) in COST:
                            side_work(v, step, b, *row, at, passed)
                        units(1000)
                for n in range(N_SHARED):
                    if reader[n] is not None:
                        reader[n] = reader[n][:3] + (reader[n][3] - 1,)

            steps(pe, step)

        @block.scalar
        def _(act):
            act.wait_ge(s_w12, 32)
            act.wait_ge(s_dconst, 1)
            act.activation(HID[0][:, :, :], W1RAW.rearrange("p c (n f) -> p (c n) f", f=256), ACT.Abs,
                           accum_out=ABS[:, 0:1]).then_inc(s_abs, 1)
            act.activation(HID[1][:, :, :], W2RAW, ACT.Abs, accum_out=ABS[:, 1:2]).then_inc(s_abs, 1)
            act.wait_ge(s_wq, 32)
            act.wait_ge(s_small, 80)
            act.activation(WQKV[0][:, :, :], WQRAW, ACT.Identity).then_inc(s_wsplit_h, 1)
            act.activation(WOUT[0][:, :, :], WORAW, ACT.Identity).then_inc(s_wsplit_h, 1)
            act.activation(B1[0:1, :], B1R, ACT.Identity).then_inc(s_wsplit_h, 1)

            def exp(b, v, i, at):
                q = 4 * b + v
                g, u = i // 3, i % 3
                if i == 0 and not (at == 0 and v < 2):
                    act.wait_ge(s_pvf, q - 1)
                if at == 0 and v == 0 and i == 0:
                    act.wait_ge(s_quant, 2)
                    act.wait_ge(s_wsplit_l, 3)
                first, n = ((0, 384), (768, 384), (1536, 512))[u]
                lo = first + n * (g % 2)
                act.wait_ge(s_stf, 12 * q + i + 1)
                act.activation(PR[:, v % 2, g // 2, lo:lo + n], PST[i % 2][:, 0:n], ACT.Exp, scale=SCALE) \
                    .then_inc(s_exp, 1)

            def side_work(v, step, b, dr, vq, at):
                name = name_of(step)
                r = b + dr
                first = at is not None and at + dr == 0
                n = BANK.get((v, step))
                G = PG[n] if n is not None else None
                if name == "xs":
                    act.wait_ge(s_x, 16 * r + 16)
                    if not first:
                        act.wait_ge(s_qkf, 4 * r)
                        act.wait_ge(s_vf, 2 * r)
                    act.activation(XT[0][:, :, :], XRAW[:, :, :], ACT.Identity).then_inc(s_xh, 1)
                elif name == "qk":
                    j = step[1]
                    act.wait_ge(s_qkf, 4 * r + j + 1)
                    if not first:
                        act.wait_ge(s_stk[2 * (j // 2)], 96 * r)
                        act.wait_ge(s_stk[2 * (j // 2) + 1], 96 * r)
                    act.activation(QK[j][0][:, :], G[:, :], ACT.Identity, bias=BQK[:, j:j + 1]) \
                        .then_inc(s_qkh, 1)
                elif name == "vp":
                    i = step[1]
                    act.wait_ge(s_vf, 2 * r + i + 1)
                    if i == 0 and not first:
                        act.wait_ge(s_va, 4 * r)
                    act.activation(VN[:, 2 * i:2 * i + 2, :].rearrange("p t d -> p (t d)"), G[:, :],
                                   ACT.Identity).then_inc(s_v, 1)
                elif name == "nmt":
                    q = 4 * r + vq
                    act.wait_ge(s_nmtf, q + 1)
                    if not (first and vq == 0):
                        act.wait_ge(s_nmin[(vq + 3) % 4], 16 * r + (0 if vq == 0 else 16))
                    act.activation(NMT[:, :], G[0:8, :], ACT.Identity).then_inc(s_nmt, 1)
                elif name == "pvb":
                    q = 4 * r + vq
                    act.wait_ge(s_pvf, q + 1)
                    if not (first and vq == 0):
                        act.wait_ge(s_utf, q)
                    act.activation(U[:, :], PUP[:, :], ACT.Identity).then_inc(s_u, 1)
                elif name == "ot":
                    i = step[1]
                    act.wait_ge(s_otf, 2 * r + i + 1)
                    if not first:
                        act.wait_ge(s_opf, 2 * r)
                    act.activation(OT[0][:, i, :], G[:, :], ACT.Identity, bias=BV[:, i:i + 1]).then_inc(s_oth, 1)
                elif name == "x1t":
                    i = step[1]
                    act.wait_ge(s_x1tf, 2 * r + i + 1)
                    if not first:
                        act.wait_ge(s_f1f, 8 * r)
                    act.activation(X1T[0][:, i, :], G[:, :], ACT.Identity).then_inc(s_x1h, 1)
                elif name == "f1":
                    hf, p = step[1], step[2]
                    act.wait_ge(s_f1f, 8 * r + 4 * hf + p + 1)
                    if not (first and hf == 0):
                        act.wait_ge(s_f2f, 2 * r + hf)
                    act.activation(HID[0][:, 2 * p:2 * p + 2, :].rearrange("p f t -> p (f t)"), G[:, :],
                                   ACT.Relu).then_inc(s_hh, 1)

            def step(b, at):
                attn = stages(at)[0]
                for v in range(QUADS):
                    for step, woven in zip(SIDE[v], WOVEN[v]):
                        for _, kind, i in woven:
                            if kind == "scores" and attn:
                                exp(b, v, i, at)
                        row = row_of(v, step, at)
                        if row is not None:
                            side_work(v, step, b, *row, at)

            steps(act, step)

        @block.vector
        def _(dve):
            dve.memset(ONES[:, :], 1.0).then_inc(s_dconst, 1)
            dve.wait_ge(s_gam, 1)
            dve.tensor_scalar(THR[:, 0:2], PG[0][:, 0:2], 1.0 / (D * FF), EPS, ALU.mult, ALU.add) \
                .then_inc(s_dconst, 1)
            dve.wait_ge(s_dconst, 2)
            dve.tensor_scalar(THR[:, 2:4], THR[:, 0:2], -0.5, None, ALU.mult).then_inc(s_dconst, 1)
            dve.wait_ge(s_dconst, 3)
            dve.tensor_scalar(THR[:, 0:2], THR[:, 0:2], 0.5, None, ALU.mult).then_inc(s_thr, 1)
            dve.wait_ge(s_wsplit_h, 3)
            dve.tensor_tensor(WQKV[1][:, :, :], WQRAW, WQKV[0][:, :, :].bitcast(F32), ALU.subtract) \
                .then_inc(s_wsplit_l, 1)
            dve.tensor_tensor(WOUT[1][:, :, :], WORAW, WOUT[0][:, :, :].bitcast(F32), ALU.subtract) \
                .then_inc(s_wsplit_l, 1)
            dve.tensor_tensor(Y[0:1, :, :].rearrange("p t d -> p (t d)"), B1R, B1[0:1, :].bitcast(F32),
                              ALU.subtract).then_inc(s_wsplit_l, 1)

            def quantise():
                dve.wait_ge(s_thr, 1)
                for i, (raw, dst) in enumerate(((W1RAW, W1Q), (W2RAW, W2Q))):
                    if i == 1:
                        dve.wait_ge(s_quant, 1)
                    tmp = QTMP if i == 0 else QTMP.rearrange("p c (n f) -> p (c n) f", f=D)
                    dve.tensor_scalar(tmp, raw, THR[:, 2 + i:3 + i], None, ALU.is_lt).then_inc(s_dconst, 1)
                    dve.wait_ge(s_dconst, 4 + i)
                    dve.scalar_tensor_tensor(dst[:, :, :], raw, THR[:, i:i + 1], tmp, ALU.is_gt, ALU.subtract) \
                        .then_inc(s_quant, 1)

            def row_max(r, v, i, first):
                g, n = i // 4, i % 4
                if i == 0 and not (first and v == 0):
                    count = in_register(dve, 4 * r + v)
                    dve.wait_ge(s_const, POOL_CONSTANTS)
                    dve.wait_ge(s_nm, count)
                a, z = (W if n == 0 else 0), (2 * W if n == NB - 1 else 3 * W)
                count = in_register(dve, 16 * (4 * r + v) + i + 1)
                dve.wait_ge(s_const, POOL_CONSTANTS)
                dve.wait_ge(s_mxf, count)
                ps = PMX[i % 2][:, 0:z - a]
                dve.tensor_tensor_reduce(ps, ps, BAND[:, a:z], 1.0, -3e38, ALU.add, ALU.max,
                                         RMAX[:, n, g:g + 1]).then_inc(s_mxr, 1)

            def neg_max(r, v, first):
                q = 4 * r + v
                dve.wait_ge(s_mxr, 16 * q + 16)
                if not (first and v == 0):
                    dve.wait_ge(s_nmtf, q)
                dve.tensor_scalar(NM[:, :, 0, :].bitcast(F32R), RMAX[:, :, :], -1.0, None, ALU.mult) \
                    .then_inc(s_nmh, 1)
                dve.wait_ge(s_nmh, q + 1)
                dve.scalar_tensor_tensor(NM[:, :, 1, :], RMAX[:, :, :], -1.0, NM[:, :, 0, :], ALU.mult,
                                         ALU.subtract).then_inc(s_nm, 1)

            def side_work(v, step, b, dr, vq, at):
                name = name_of(step)
                r = b + dr
                first = at is not None and at + dr == 0
                n = BANK.get((v, step))
                G = PG[n] if n is not None else None
                if name == "qk":
                    j = step[1]
                    dve.wait_ge(s_qkh, 4 * r + j + 1)
                    dve.scalar_tensor_tensor(QK[j][1][:, :], G[:, :], BQK[:, j:j + 1],
                                             QK[j][0][:, :].bitcast(F32), ALU.add, ALU.subtract) \
                        .then_inc(s_qkl, 1)
                elif name == "ut":
                    q = 4 * r + vq
                    dve.wait_ge(s_utf, q + 1)
                    if not (first and vq == 0):
                        dve.wait_ge(s_on, q)
                    sums = G[:, :].rearrange("p (a e) -> p a e", e=32)
                    dve.reciprocal(RC[:, :], sums[:, :, 16]).then_inc(s_rc, 1)
                    dve.wait_ge(s_rc, q + 1)
                    if vq == 0 and not first:
                        dve.wait_ge(s_otf, 2 * r)
                    dve.tensor_tensor(ON[:, :, 64 * vq:64 * vq + 64].rearrange("p t (g d) -> p t g d", g=4),
                                      sums[:, :, 0:16].rearrange("p (t g) d -> p t g d", t=TB),
                                      RC[:, :].rearrange("p (t g) -> p t g", t=TB)[:, :, :, None]
                                      .to_broadcast([P, TB, 4, DH]), ALU.mult).then_inc(s_on, 1)
                elif name == "ot":
                    i = step[1]
                    dve.wait_ge(s_oth, 2 * r + i + 1)
                    dve.scalar_tensor_tensor(OT[1][:, i, :], G[:, :], BV[:, i:i + 1], OT[0][:, i, :].bitcast(F32),
                                             ALU.add, ALU.subtract) \
                        .then_inc(s_otl, 1)
                elif name == "op":
                    i = step[1]
                    dve.wait_ge(s_opf, 2 * r + i + 1)
                    dve.wait_ge(s_xrb, r + 1)
                    y = Y[:, 2 * i:2 * i + 2, :]
                    dve.tensor_tensor(y, G[:, :].rearrange("p (t d) -> p t d", t=2), y, ALU.add) \
                        .then_inc(s_y, 1)
                elif name == "ln1":
                    if not first:
                        dve.wait_ge(s_mv2, 4 * r)
                        dve.wait_ge(s_x1, 4 * r)
                    for t in range(TB):
                        dve.wait_ge(s_y, 2 * r + 1 + t // 2)
                        dve.bn_stats(ST[:, t, :], Y[:, t, :]).then_inc(s_st1, 1)
                    for t in range(TB):
                        count = in_register(dve, 4 * r + 1 + t)
                        dve.wait_ge(s_thr, 1)
                        dve.wait_ge(s_st1, count)
                        dve.bn_aggr(MV1[:, t, :], ST[:, t, :]).then_inc(s_mv1, 1)
                elif name == "x1t":
                    i = step[1]
                    dve.wait_ge(s_x1h, 2 * r + i + 1)
                    dve.tensor_tensor(X1T[1][:, i, :], G[:, :], X1T[0][:, i, :].bitcast(F32), ALU.subtract) \
                        .then_inc(s_x1l, 1)
                elif name == "f1":
                    hf, p = step[1], step[2]
                    dve.wait_ge(s_hh, 8 * r + 4 * hf + p + 1)
                    pair = [h[:, 2 * p:2 * p + 2, :].rearrange("p f t -> p (f t)") for h in HID]
                    dve.scalar_tensor_tensor(pair[1], G[:, :], 0.0, pair[0].bitcast(F32), ALU.max,
                                             ALU.subtract).then_inc(s_hl, 1)
                elif name == "f2":
                    hf = step[1]
                    dve.wait_ge(s_f2f, 2 * r + hf + 1)
                    dve.wait_ge(s_x1b, r + 1)
                    z = X1[:, 2 * hf:2 * hf + 2, :]
                    dve.tensor_tensor(z, G[:, :].rearrange("p (t d) -> p t d", t=2), z, ALU.add) \
                        .then_inc(s_z, 1)
                elif name == "ln2":
                    hf = step[1]
                    dve.wait_ge(s_mv1, 4 * r + 4)
                    if not first:
                        dve.wait_ge(s_o, 4 * r)
                    dve.wait_ge(s_z, 2 * r + hf + 1)
                    for t in (2 * hf, 2 * hf + 1):
                        dve.bn_stats(ST[:, t, :], X1[:, t, :]).then_inc(s_st2, 1)
                    for t in (2 * hf, 2 * hf + 1):
                        count = in_register(dve, 4 * r + 1 + t)
                        dve.wait_ge(s_thr, 1)
                        dve.wait_ge(s_st2, count)
                        dve.bn_aggr(MV2[:, t, :], ST[:, t, :]).then_inc(s_mv2, 1)

            def step(b, at):
                if at == 0:
                    quantise()
                for v in range(QUADS):
                    q = max_quad(v, at)
                    for kind, what in dve_order(v):
                        if kind == "max":
                            if q is not None:
                                row_max(b + q[0], q[1], what, at == -1)
                                if what == MAX_UNITS - 1:
                                    neg_max(b + q[0], q[1], at == -1)
                        else:
                            row = row_of(v, what, at)
                            if row is not None:
                                side_work(v, what, b, *row, at)

            steps(dve, step)

        @block.gpsimd
        def _(pool):
            pool.memset(IDN[:, :], 0.0).then_inc(s_const, 1)
            pool.memset(BAND[:, :], 0.0).then_inc(s_const, 1)
            pool.wait_ge(s_const, 2)
            pool.affine_select(out=IDN[:, :], in_=IDN[:, :], compare_op=ALU.not_equal, fill=1.0, base=0,
                               pattern=[[-1, P]], channel_multiplier=1).then_inc(s_const, 1)
            pool.affine_select(out=BAND[:, 0:W], in_=BAND[:, 0:W], compare_op=ALU.is_ge, fill=MASKED, base=0,
                               pattern=[[1, W]], channel_multiplier=-1).then_inc(s_const, 1)
            pool.affine_select(out=BAND[:, 2 * W:3 * W], in_=BAND[:, 2 * W:3 * W], compare_op=ALU.is_ge,
                               fill=MASKED, base=0, pattern=[[-1, W]], channel_multiplier=1) \
                .then_inc(s_const, 1)

            pool.memset(HALF[:, :], -0.5).then_inc(s_const, 1)
            pool.memset(ONES2[:, :].bitcast(F32), 1.0).then_inc(s_const, 1)
            pool.memset(SK[:, :, :].bitcast(F32), 1.0).then_inc(s_const, 1)
            pool.memset(VAUG[:, :, :, :, :], 1.0).then_inc(s_const, 1)
            pool.wait_ge(s_const, POOL_CONSTANTS)

            def mask(b, v, g):
                count = in_register(pool, 3 * (16 * b + 4 * v + g) + 3)
                pool.wait_ge(s_const, POOL_CONSTANTS)
                pool.wait_ge(s_exp, count)
                pr = PR[:, v % 2, g // 2, :]
                inner = pr[:, 0:1536].rearrange("p (m w) -> p m w", w=384)
                outer = pr[:, 1536:2560].rearrange("p (h w) -> p h w", w=512)
                for pr_before, n in ((inner[:, :, 0:W], 4), (outer[:, :, 0:W], 2)):
                    pool.affine_select(out=pr_before, in_=pr_before, compare_op=ALU.is_ge, fill=0.0, base=0,
                                       pattern=[[0, n], [1, W]], channel_multiplier=-1)
                for pr_after, n in ((inner[:, :, 2 * W:3 * W], 4), (outer[:, :, 3 * W:4 * W], 2)):
                    last = pool.affine_select(out=pr_after, in_=pr_after, compare_op=ALU.is_ge, fill=0.0, base=0,
                                              pattern=[[0, n], [-1, W]], channel_multiplier=1)
                last.then_inc(s_mask, 1)

            def v_in_place(r, v, first):
                count = in_register(pool, 4 * (r - 1) + v + 1)
                made = in_register(pool, 2 * r + 2)
                pool.wait_ge(s_const, POOL_CONSTANTS)
                pool.wait_ge(s_v, made)
                if not first:
                    pool.wait_ge(s_pvf, count)
                pool.tensor_copy(VAUG[:, v, :, :, 0:DH],
                                 VN[:, :, 64 * v:64 * v + 64].rearrange("p t (g d) -> p t g d", g=4)) \
                    .then_inc(s_va, 1)

            def side_work(v, step, b, dr, vq, at):
                name = name_of(step)
                r = b + dr
                first = at is not None and at + dr == 0
                if name == "xs":
                    pool.wait_ge(s_xh, r + 1)
                    pool.tensor_tensor(XT[1][:, :, :], XRAW[:, :, :], XT[0][:, :, :].bitcast(F32),
                                       ALU.subtract).then_inc(s_xl, 1)
                elif name == "ot" and step[1] == 0:
                    pool.wait_ge(s_xr, 16 * r + 16)
                    pool.tensor_tensor(Y[:, :, :], Y[:, :, :], BOUT[:, None, :].to_broadcast([P, TB, D]),
                                       ALU.add).then_inc(s_xrb, 1)
                elif name == "ln1":
                    count = in_register(pool, 4 * r + 4)
                    pool.wait_ge(s_const, POOL_CONSTANTS)
                    pool.wait_ge(s_mv1, count)
                    pool.tensor_scalar(VE[:, :], MV1[:, :, 1], 1.0, EPS, ALU.mult, ALU.add).then_inc(s_ve, 1)
                    pool.wait_ge(s_ve, 3 * r + 1)
                    pool.tensor_tensor(RS1[:, :], VE[:, :], HALF[:, :], ALU.pow).then_inc(s_rs1, 1)
                    count = in_register(pool, r + 1)
                    stored = in_register(pool, 32 * r) if not first else None
                    pool.wait_ge(s_const, POOL_CONSTANTS)
                    pool.wait_ge(s_rs1, count)
                    if not first:
                        pool.wait_ge(s_od, stored)
                    for t in range(TB):
                        pool.tensor_scalar(X1[:, t, :], Y[:, t, :], MV1[:, t, 0:1], RS1[:, t:t + 1],
                                           ALU.subtract, ALU.mult).then_inc(s_x1, 1)
                elif name == "x1t" and step[1] == 1:
                    pool.wait_ge(s_x1tf, 2 * r + 2)
                    pool.tensor_tensor(X1[:, :, :], X1[:, :, :], B2[:, None, :].to_broadcast([P, TB, D]),
                                       ALU.add).then_inc(s_x1b, 1)
                elif name == "ln2":
                    hf = step[1]
                    two = slice(2 * hf, 2 * hf + 2)
                    count = in_register(pool, 4 * r + 2 * hf + 2)
                    pool.wait_ge(s_const, POOL_CONSTANTS)
                    pool.wait_ge(s_mv2, count)
                    pool.tensor_scalar(VE[:, two], MV2[:, two, 1], 1.0, EPS, ALU.mult, ALU.add).then_inc(s_ve, 1)
                    pool.wait_ge(s_ve, 3 * r + 2 + hf)
                    pool.tensor_tensor(RS2[:, two], VE[:, two], HALF[:, two], ALU.pow).then_inc(s_rs2, 1)
                    count = in_register(pool, 2 * r + hf + 1)
                    pool.wait_ge(s_const, POOL_CONSTANTS)
                    pool.wait_ge(s_rs2, count)
                    for t in (2 * hf, 2 * hf + 1):
                        pool.tensor_scalar(X1[:, t, :], X1[:, t, :], MV2[:, t, 0:1], RS2[:, t:t + 1],
                                           ALU.subtract, ALU.mult).then_inc(s_o, 1)

            def step(b, at):
                attn = stages(at)[0]
                for v in range(QUADS):
                    if v == 0 and attn:
                        for vq in range(3):
                            v_in_place(b, vq, at == 0)
                    for step, woven in zip(SIDE[v], WOVEN[v]):
                        if attn:
                            for _, kind, i in woven:
                                if kind == "scores" and i in (5, 11):
                                    mask(b, v, i // 3)
                            if v == 0 and step == "ut":
                                v_in_place(b, 3, at == 0)
                        row = row_of(v, step, at)
                        if row is not None:
                            side_work(v, step, b, *row, at)

            steps(pool, step)


def kernel(L0_attn_x, L0_attn_Wqkv, L0_attn_bqkv, L0_attn_Wout, L0_attn_bout, L0_ffn_W1, L0_ffn_b1,
           L0_ffn_W2, L0_ffn_b2):
    import numpy as np
    from concourse import bacc
    from concourse.bass_utils import run_bass_kernel_spmd

    x = np.ascontiguousarray(L0_attn_x)
    wqkv = np.asarray(L0_attn_Wqkv)
    bqkv = np.asarray(L0_attn_bqkv)
    order = np.arange(2 * D).reshape(2, 2, 2, 4, DH).transpose(1, 0, 2, 4, 3).reshape(-1)
    arrays = {
        "x": x,
        "xT": np.ascontiguousarray(x.transpose(0, 2, 1)),
        "wqkv": np.ascontiguousarray(np.concatenate([wqkv[:, order], wqkv[:, 2 * D:]], axis=1)),
        "bqk": np.ascontiguousarray(bqkv[order].reshape(4, P).T),
        "bv": np.ascontiguousarray(bqkv[2 * D:].reshape(KC, P).T),
        "wout": np.ascontiguousarray(L0_attn_Wout),
        "bout": np.ascontiguousarray(L0_attn_bout),
        "w1T": np.ascontiguousarray(np.asarray(L0_ffn_W1).T),
        "b1": np.ascontiguousarray(L0_ffn_b1),
        "w2T": np.ascontiguousarray(np.asarray(L0_ffn_W2).T),
        "b2": np.ascontiguousarray(L0_ffn_b2),
    }
    nc = bacc.Bacc("TRN2", target_bir_lowering=False, num_devices=1)
    aps = {n: nc.dram_tensor(f"in_{n}", a.shape, mybir.dt.from_np(a.dtype), kind="ExternalInput").ap()
           for n, a in arrays.items()}
    out = nc.dram_tensor("out", (B, S, D), F32, kind="ExternalOutput").ap()
    postln_layer(nc, out=out, **aps)
    result = run_bass_kernel_spmd(nc, [{f"in_{n}": a for n, a in arrays.items()}], core_ids=[0])
    return result.results[0]["out"]
```

```python
from contextlib import ExitStack

import concourse.bass as bass
from concourse import mybir

F32 = mybir.dt.float32
F32R = mybir.dt.float32r
ALU = mybir.AluOpType
ACT = mybir.ActivationFunctionType

P = 128
B, S, D = 16, 512, 256
H, DH, W = 16, 16, 128
FF = 1024
NB = S // W
KC = D // P
FC = FF // P
QUADS = H // 4
TB = S // P
EPS = 1e-5
SCALE = 1.0 / 16.0
MASKED = -1e30
CONSTANTS = 8

PCOL = {1: (0, 384, 0, 384), 2: (768, 384, 128, 384), 3: (1536, 512, 256, 256), 0: (1792, 512, 0, 256)}
PW = 2560

SIDE = [
    [("qk", 0), "nmt", "pva", "pvb", "ut", ("vp", 0), ("ot", 0), ("ot", 1), ("qk", 1), ("qk", 2), ("op", 0),
     ("op", 1)],
    [("ln1", 0), ("ln1", 1), ("ln1", 2), ("vp", 1), "nmt", ("ln1", 3), "pva", "pvb", ("x1", 0), ("x1", 1),
     ("x1", 2), ("x1", 3), ("qk", 3), ("x1t", 0), ("x1t", 1), "ut", ("f1", 0, 0)],
    [("f1", 0, 1), ("xs", 0), ("f1", 0, 2), ("f1", 0, 3), ("xs", 1), "pva", "nmt", "pvb", ("f2", 0), "ut",
     ("f1", 1, 0)],
    [("f1", 1, 1), "nmt", "xr", ("ln2", 0), ("ln2", 1), ("f1", 1, 2), "pva", "pvb", ("f1", 1, 3), "ut", ("f2", 1),
     ("ln2", 2), ("ln2", 3)],
]
COST = {"qk": (3072, 6), "vp": (3072, 12), "op": (3072, 12), "ut": (1024, 4), "ot": (1024, 4), "x1t": (1024, 4),
        "nmt": (256, 1), "f1": (2560, 10), "f2": (8192, 32), "pva": (3200, 2), "pvb": (3200, 2)}
UNITS = 12
BLOCKS = ((1,), (2,), (3, 0))
N_MAX = 3
SCORES_AT = (0.72, 0.88)
MAXIMA_AT = (0.36, 0.88)
LAG = {"ln1": 1, "ln2": 1, "qk": 1, "ot": 1, "x1t": 0, "f1": 0, "op": 1, "ut": 0, "f2": 1}
N_SHARED = 6 - N_MAX

USES_BANK = {"pva", "ut", "qk", "ot", "op", "vp", "x1t", "f1", "f2", "nmt"}
POST = {"ot", "op", "ln1", "x1", "x1t", "f1", "f2", "ln2"}


def name_of(step):
    return step if isinstance(step, str) else step[0]


def banks():
    out, n = {}, 0
    for v in range(QUADS):
        for step in SIDE[v]:
            if name_of(step) in USES_BANK:
                out[(v, step)] = n % N_SHARED
                n += 1
        out[(v, "pvb")] = out[(v, "pva")]
    return out


NEEDS = {"ot": "ut", "op": "ot", "f1": "x1t", "f2": "f1"}


def weave():
    out = []
    for v in range(QUADS):
        total = sum(COST.get(name_of(s), (0, 0))[0] for s in SIDE[v])
        units = [((i + SCORES_AT[0]) / UNITS * total * SCORES_AT[1], "scores", i) for i in range(UNITS)]
        units += [((i + MAXIMA_AT[0]) / UNITS * total * MAXIMA_AT[1], "max", i) for i in range(UNITS)]
        units.sort()
        at, slot = 0, []
        for s in SIDE[v]:
            cost, places = COST.get(name_of(s), (0, 0))
            slot.append([(int((pos - at) / cost * places), kind, i)
                         for pos, kind, i in units if cost and at <= pos < at + cost])
            at += cost
        out.append(slot)
    return out


BANK = banks()
WOVEN = weave()


def stages(at):
    if at is None:
        return True, True, True, True
    return 0 <= at < B, 1 <= at <= B, 0 <= at + 1 < B, 0 <= at + 2 < B


def row_of(v, step, at):
    attn, post, nxt, nxt2 = stages(at)
    name = name_of(step)
    if name in POST:
        return (-1, None) if post else None
    if name in ("qk", "vp"):
        return (1, None) if nxt else None
    if name == "xs":
        return (2, None) if nxt2 else None
    if name == "xr":
        return (0, None) if attn else None
    if name == "nmt":
        if v < 3:
            return (0, v + 1) if attn else None
        return (1, 0) if nxt else None
    if v == 0:
        return (-1, 3) if post else None
    return (0, v - 1) if attn else None


def max_quad(v, at):
    attn, _, nxt, _ = stages(at)
    if v < 2:
        return (0, v + 2) if attn else None
    return (1, v - 2) if nxt else None


def dve_order(v):
    out, late, maxima = [], [], 0

    def due(now):
        while late and late[0][0] <= now:
            out.append(("side", late.pop(0)[1]))

    for step, woven in zip(SIDE[v], WOVEN[v]):
        while late and (any(name_of(s) == NEEDS.get(name_of(step)) for _, s in late)
                        or name_of(step) in USES_BANK and len(late) >= N_SHARED):
            out.append(("side", late.pop(0)[1]))
        for _, kind, i in woven:
            if kind == "max":
                out.append(("max", i))
                maxima += 1
                due(maxima)
        after = late[-1][0] + 1 if late and name_of(late[-1][1]) == name_of(step) in ("ln1", "ln2") else 0
        late.append((max(maxima + LAG.get(name_of(step), 0), after), step))
        due(maxima)
    due(UNITS + 100)
    return out


def steps(eng, step):
    for at in (-2, -1, 0, 1):
        step(at, at)
    with eng.Fori(2, B - 2) as b:
        step(b, None)
    for at in (B - 2, B - 1, B):
        step(at, at)


def in_register(eng, count):
    if isinstance(count, int):
        return count
    reg = eng.alloc_register()
    eng.reg_mov(reg, count)
    return eng.snap(reg)


def postln_layer(nc, xT, x, wqkv, bqk, bv, wout, bout, w1T, b1, w2T, b2, out):
    ctx = ExitStack()
    with ctx:
        def sb(name, shape, dt=F32):
            return ctx.enter_context(nc.sbuf_tensor(name, shape, dt))

        def sem(name):
            return ctx.enter_context(nc.semaphore(name))

        WQKV = [sb("wqkv_hi", [P, KC, 3 * D], F32R), sb("wqkv_lo", [P, KC, 3 * D], F32R)]
        WOUT = [sb("wout_hi", [P, KC, D], F32R), sb("wout_lo", [P, KC, D], F32R)]
        W1Q = sb("w1q", [P, KC, FF], F32R)
        W2Q = sb("w2q", [P, FC, D], F32R)
        B1 = sb("b1_rows", [2, FF], F32R)
        ONES2 = sb("ones_rows", [2, S // 2], F32R)
        BQK = sb("bqk", [P, 4])
        BV = sb("bv_cols", [P, KC])
        BOUT = sb("bout_rep", [P, D])
        B2 = sb("b2_rep", [P, D])
        IDN = sb("identity", [P, P])
        ONES = sb("ones", [P, P])
        BAND = sb("band", [P, 3 * W])
        XRAW = sb("x_raw", [P, KC, S])
        XT = [sb("xT_hi", [P, KC, S], F32R), sb("xT_lo", [P, KC, S], F32R)]
        QK = [[sb(f"qk{j}_hi", [P, S], F32R), sb(f"qk{j}_lo", [P, S], F32R)] for j in range(4)]
        SQ = sb("q_stack", [P, 8, S], F32R)
        SK = sb("k_stack", [P, 8, S], F32R)
        VN = sb("v_next", [P, TB, D])
        VAUG = sb("v_aug", [P, QUADS, TB, 4, 32])
        PR = sb("probs", [P, 2, 2, PW])
        U = sb("u", [P, S])
        RC = sb("recip", [P, TB * 4])
        ON = sb("o_norm", [P, TB, D])
        OT = [sb("oT_hi", [P, KC, S], F32R), sb("oT_lo", [P, KC, S], F32R)]
        Y = sb("y", [P, TB, D])
        X1 = sb("x1", [P, TB, D])
        X1T = [sb("x1T_hi", [P, KC, S], F32R), sb("x1T_lo", [P, KC, S], F32R)]
        HID = [sb("hid_hi", [P, FC, S // 2], F32R), sb("hid_lo", [P, FC, S // 2], F32R)]
        RMAX = sb("rmax", [P, 4, NB])
        NM = sb("neg_max", [P, 2, 4, NB])
        NMT = sb("neg_maxT", [8 * NB, 2, W], F32R)
        ST = sb("ln_stats", [P, TB, 6])
        MV1 = sb("ln1_mv", [P, TB, 2])
        MV2 = sb("ln2_mv", [P, TB, 2])
        VE = sb("var_eps", [P, TB])
        HALF = sb("minus_half", [P, TB])
        RS1 = sb("ln1_rstd", [P, TB])
        NEG1 = sb("ln1_neg_mean", [P, TB])
        NMR1 = sb("ln1_neg_mean_rstd", [P, TB])
        RS2 = sb("ln2_rstd", [P, TB])
        ABS = sb("abs_sums", [P, 3])
        THR = sb("thresholds", [P, 4])

        def bank(name):
            return ctx.enter_context(nc.psum_tensor(name, [P, 512], F32))

        PST = [bank("st_a"), bank("st_b")]
        PMX = [bank(f"mx{i}") for i in range(N_MAX)]
        PG = [bank(f"shared{n}") for n in range(N_SHARED)]

        FLAT = "p c n -> p (c n)"
        PRF = PR[:, 1].rearrange("p g w -> p (g w)")
        HALF_W = KC * FF // 2
        WQRAW = PRF[:, 0:KC * 3 * D].rearrange("p (c n) -> p c n", c=KC)
        WORAW = PRF[:, KC * 3 * D:KC * 4 * D].rearrange("p (c n) -> p c n", c=KC)
        W1RAW = [X1[:, :, :].rearrange(FLAT), ON[:, :, :].rearrange(FLAT)]
        W2AT = KC * 4 * D
        W2RAW = [PRF[:, W2AT + HALF_W * k:W2AT + HALF_W * (k + 1)] for k in range(2)]
        B1R = PRF[0:1, W2AT + 2 * HALF_W:W2AT + 2 * HALF_W + FF]
        QTMP = X1T[0][:, :, :].rearrange(FLAT)
        QUANTISED = [(1, 0), (1, 1), (0, 1), (0, 0)]

        s_wq = sem("wqkv_in")
        s_w1 = sem("w1_in")
        s_w2 = sem("w2_in")
        s_small = sem("bqk_bv_in")
        s_const = sem("constants")
        s_blank = sem("blank_constants")
        s_dconst = sem("threshold_steps")
        s_wo = sem("wout_b1_in")
        s_b2 = sem("bout_b2_in")
        s_b1 = sem("b1_lo_in")
        s_abs = sem("abs_sums_done")
        s_gam = sem("abs_totals_full")
        s_thr = sem("thresholds_done")
        s_wsplit_h = sem("weights_hi")
        s_wsplit_l = sem("weights_lo")
        s_quant = sem("weights_quantised")
        s_x = sem("x_in")
        s_xh = sem("xT_hi_done")
        s_xl = sem("xT_lo_done")
        s_qkf = sem("qk_full")
        s_qkh = sem("qk_hi_done")
        s_qkl = sem("qk_lo_done")
        s_vf = sem("v_full")
        s_v = sem("v_next_done")
        s_va = sem("v_aug_done")
        s_stk = [sem(f"stack_in{v}") for v in range(4)]
        s_mxf = sem("max_scores_full")
        s_mxr = sem("max_read")
        s_nmh = sem("neg_max_hi")
        s_nm = sem("neg_max_done")
        s_nmtf = sem("neg_maxT_full")
        s_nmt = sem("neg_maxT_done")
        s_nmin = [sem(f"neg_max_in{v}") for v in range(4)]
        s_stf = sem("scores_full")
        s_exp = sem("exp_done")
        s_mask = sem("mask_done")
        s_pvf = sem("pv_full")
        s_u = sem("u_done")
        s_utf = sem("uT_full")
        s_rc = sem("recip_done")
        s_on = sem("o_norm_done")
        s_otf = sem("oT_full")
        s_oth = sem("oT_hi_done")
        s_otl = sem("oT_lo_done")
        s_xr = sem("x_residual_in")
        s_xrb = sem("x_residual_biased")
        s_opf = sem("out_proj_full")
        s_y = sem("y_done")
        s_st1 = sem("ln1_stats_done")
        s_mv1 = sem("ln1_mv_done")
        s_ve = sem("var_eps_done")
        s_rs1 = sem("ln1_rstd_done")
        s_nmr = sem("neg_mean_rstd")
        s_x1 = sem("x1_done")
        s_x1tf = sem("x1T_full")
        s_x1h = sem("x1T_hi_done")
        s_x1l = sem("x1T_lo_done")
        s_x1b = sem("x1_biased")
        s_f1f = sem("ffn1_full")
        s_hh = sem("hidden_hi_done")
        s_hl = sem("hidden_lo_done")
        s_f2f = sem("ffn2_full")
        s_z = sem("z_done")
        s_st2 = sem("ln2_stats_done")
        s_mv2 = sem("ln2_mv_done")
        s_rs2 = sem("ln2_rstd_done")
        s_o = sem("out_done")
        s_od = sem("out_stored")

        block = ctx.enter_context(nc.Block())

        @block.sync
        def _(sp):
            sp.dma_start(WQRAW, wqkv.rearrange("(c p) n -> p c n", p=P)).then_inc(s_wq, 16)
            sp.dma_start(BQK[:, :], bqk).then_inc(s_small, 16)
            sp.dma_start(BV[:, :], bv).then_inc(s_small, 16)

            def more_weights():
                for k in range(2):
                    sp.dma_start(W1RAW[k], w1T[P * k:P * k + P]).then_inc(s_w1, 16)
                w2_place = PRF[:, W2AT:W2AT + 2 * HALF_W].rearrange("p (c n) -> p c n", c=FC)
                sp.dma_start(w2_place, w2T.rearrange("(c p) n -> p c n", p=P)).then_inc(s_w2, 16)
                sp.dma_start(WORAW, wout.rearrange("(c p) n -> p c n", p=P)).then_inc(s_wo, 16)
                sp.dma_start(B1R, b1[None, :]).then_inc(s_wo, 16)
                sp.dma_start(BOUT[:, :], bout[None, :].to_broadcast([P, D])).then_inc(s_b2, 16)
                sp.dma_start(B2[:, :], b2[None, :].to_broadcast([P, D])).then_inc(s_b2, 16)

            def stack(r, v, first):
                c, ih = v // 2, v % 2
                sp.wait_ge(s_qkh, 4 * r + 2 * c + 2)
                sp.wait_ge(s_qkl, 4 * r + 2 * c + 2)
                if not first:
                    sp.wait_ge(s_stf, 12 * (4 * r - 4 + v) + 12)
                half = slice(64 * ih, 64 * ih + 64)
                heads = slice(4 * ih, 4 * ih + 4)
                for dst, j, terms in ((SQ, 2 * c, (0, 1, 0)), (SK, 2 * c + 1, (0, 0, 1))):
                    for t, part in enumerate(terms):
                        rows = slice(64 * c + 16 * t, 64 * c + 16 * t + 16)
                        sp.dma_start(dst[rows, heads, :].bitcast(F32), QK[j][part][half, :].bitcast(F32)).then_inc(s_stk[v], 16)

            def step(b, at):
                attn, post, nxt, nxt2 = stages(at)
                if nxt2:
                    if at != -2:
                        sp.wait_ge(s_xl, b + 2)
                    sp.dma_start(XRAW[:, :, :], xT[bass.ds(b + 2, 1)].rearrange("a (c p) t -> p (a c) t", p=P)) \
                        .then_inc(s_x, 16)
                if at == -2:
                    more_weights()
                    sp.wait_ge(s_const, CONSTANTS)
                if at == 0:
                    sp.wait_ge(s_wsplit_l, 3)
                    sp.dma_start(B1[1:2, :].bitcast(F32), Y[0:1, :, :].rearrange("p t d -> p (t d)")) \
                        .then_inc(s_b1, 16)
                for v in range(QUADS):
                    if v == 0 and attn:
                        stack(b, 3, at == 0)
                    if v > 0 and nxt:
                        stack(b + 1, v - 1, at == -1)
                    if v == 3 and post:
                        store(b, 0)
                    if v == 2 and attn:
                        if at == 0:
                            sp.wait_ge(s_b1, 16)
                        else:
                            sp.wait_ge(s_x1, 4 * b)
                        sp.dma_start(Y[:, :, :], x[bass.ds(b, 1)].rearrange("a (t p) d -> p (a t) d", p=P)) \
                            .then_inc(s_xr, 16)
                    q = row_of(v, "nmt", at)
                    if q is not None:
                        r, vq = b + q[0], q[1]
                        sp.wait_ge(s_nmt, 4 * r + vq + 1)
                        c, ih = vq // 2, vq % 2
                        rows = SQ[64 * c + 48:64 * c + 50, 4 * ih:4 * ih + 4, :].bitcast(F32)
                        sp.dma_start(rows.rearrange("a g (n q) -> a (g n) q", n=NB), NMT[:, vq % 2].bitcast(F32)).then_inc(s_nmin[vq], 16)
                if post:
                    store(b, 1)

            def store(b, hf):
                sp.wait_ge(s_o, 4 * (b - 1) + 2 * hf + 2)
                sp.dma_start(out[bass.ds(b - 1, 1), 256 * hf:256 * hf + 256].rearrange("a (t p) d -> p (a t) d", p=P),
                             X1[:, 2 * hf:2 * hf + 2, :]).then_inc(s_od, 16)

            steps(sp, step)
            sp.wait_ge(s_od, 32 * B)

        @block.tensor
        def _(pe):
            pe.wait_ge(s_const, CONSTANTS)
            pe.wait_ge(s_wsplit_h, 1)
            pe.wait_ge(s_wsplit_l, 1)

            def weight_totals():
                pe.wait_ge(s_abs, 3)
                pe.matmul(PMX[0][:, 0:2], ONES[:, :], ABS[:, 0:2], start=True, stop=False)
                pe.matmul(PMX[0][:, 0:1], ONES[:, :], ABS[:, 2:3], start=False, stop=True).then_inc(s_gam, 1)
                pe.wait_ge(s_thr, 1)

            reader = [None] * N_SHARED

            def bank_free(n, b):
                if reader[n] is not None:
                    s, per_row, count, dr = reader[n]
                    pe.wait_ge(s, per_row * (b + dr) + count)
                return PG[n]

            def scores(b, v, i, at):
                g, u = i // 3, i % 3
                c, hd = v // 2, 4 * (v % 2) + g
                rows = slice(64 * c, 64 * c + 50)
                if i == 0:
                    pe.wait_ge(s_stk[v], 96 * b + 96)
                    pe.wait_ge(s_nmin[v], 16 * b + 16)
                if not (at == 0 and v == 0 and i < 2):
                    pe.wait_ge(s_exp, 12 * (4 * b + v) + i - 1)
                for m in BLOCKS[u]:
                    _, _, q0, n = PCOL[m]
                    col = n * (m == 0)
                    mm = pe.matmul(PST[i % 2][:, col:col + n], SK[rows, hd, W * m:W * m + W],
                                   SQ[rows, hd, q0:q0 + n], start=True, stop=True)
                mm.then_inc(s_stf, 1)

            def max_scores(r, v, i, first):
                g, u = i // 3, i % 3
                c, hd = v // 2, 4 * (v % 2) + g
                rows = slice(64 * c, 64 * c + 48)
                if i == 0:
                    pe.wait_ge(s_stk[v], 96 * r + 96)
                if not (first and v == 0 and i < N_MAX):
                    pe.wait_ge(s_mxr, 12 * (4 * r + v) + i - N_MAX + 1)
                for m in BLOCKS[u]:
                    _, _, k0, n = PCOL[m]
                    col = n * (m == 0)
                    mm = pe.matmul(PMX[i % N_MAX][:, col:col + n], SQ[rows, hd, W * m:W * m + W],
                                   SK[rows, hd, k0:k0 + n], start=True, stop=True)
                mm.then_inc(s_mxf, 1)

            def split3(ps, lhs, rhs, passed):
                terms = [(a, z, kc) for kc in range(KC) for a, z in ((0, 0), (1, 0), (0, 1))]
                for n, (a, z, kc) in enumerate(terms):
                    passed()
                    mm = pe.matmul(ps, lhs(a, kc), rhs(z, kc), start=(n == 0), stop=(n == len(terms) - 1))
                return mm

            def side_work(v, step, b, dr, vq, at, passed):
                name = name_of(step)
                r = b + dr
                first = at is not None and at + dr == 0
                G, n = None, BANK.get((v, step))
                if n is not None:
                    G = PG[n] if name == "pvb" else bank_free(n, b)
                if name == "pva" or name == "pvb":
                    q = 4 * r + vq
                    if name == "pva":
                        pe.wait_ge(s_mask, 2 * q + 2)
                        pe.wait_ge(s_va, q + 1)
                    for m in ((0, 1) if name == "pva" else (2, 3)):
                        passed()
                        col, pitch, q0, width = PCOL[m]
                        for g in range(4):
                            lo = col + pitch * (g % 2)
                            mm = pe.matmul(G[32 * g:32 * g + 32, q0:q0 + width], VAUG[:, vq, m, g, :],
                                           PR[:, vq % 2, g // 2, lo:lo + width], start=(m == 0), stop=(m == 3),
                                           skip_group_check=True)
                    if name == "pvb":
                        mm.then_inc(s_pvf, 1)
                        reader[n] = (s_u, 4, vq + 1, dr)
                elif name == "ut":
                    pe.wait_ge(s_u, 4 * r + vq + 1)
                    for t in range(TB):
                        passed()
                        mm = pe.transpose(G[:, P * t:P * t + P], U[:, P * t:P * t + P], IDN[:, :])
                    mm.then_inc(s_utf, 1)
                    reader[n] = (s_on, 4, vq + 1, dr)
                elif name == "nmt":
                    pe.wait_ge(s_nm, 4 * r + vq + 1)
                    pe.transpose(G[0:8 * NB, 0:W], NM[:, :, :, :].rearrange("p a g n -> p (a g n)"), IDN[:, :]) \
                        .then_inc(s_nmtf, 1)
                    reader[n] = (s_nmt, 4, vq + 1, dr)
                elif name == "qk":
                    j = step[1]
                    if j == 0:
                        pe.wait_ge(s_xh, 2 * r + 2)
                        pe.wait_ge(s_xl, r + 1)
                    cols = slice(P * j, P * j + P)
                    split3(G[:, :], lambda a, kc: WQKV[a][:, kc, cols], lambda z, kc: XT[z][:, kc, :], passed) \
                        .then_inc(s_qkf, 1)
                    reader[n] = (s_qkl, 4, j + 1, dr)
                elif name == "vp":
                    i = step[1]
                    for t in (2 * i, 2 * i + 1):
                        mm = split3(G[:, D * (t % 2):D * (t % 2) + D],
                                    lambda a, kc: XT[a][:, kc, P * t:P * t + P],
                                    lambda z, kc: WQKV[z][:, kc, 2 * D:3 * D], passed)
                    mm.then_inc(s_vf, 1)
                    reader[n] = (s_v, 2, i + 1, dr)
                elif name == "ot":
                    i = step[1]
                    pe.wait_ge(s_on, 4 * r + 4)
                    for t in range(TB):
                        passed()
                        mm = pe.transpose(G[:, P * t:P * t + P], ON[:, t, P * i:P * i + P], IDN[:, :])
                    mm.then_inc(s_otf, 1)
                    reader[n] = (s_otl, 2, i + 1, dr)
                elif name == "op":
                    i = step[1]
                    pe.wait_ge(s_oth, 2 * r + 2)
                    pe.wait_ge(s_otl, 2 * r + 2)
                    if first and i == 0:
                        pe.wait_ge(s_wsplit_h, 2)
                        pe.wait_ge(s_wsplit_l, 2)
                    for t in (2 * i, 2 * i + 1):
                        mm = split3(G[:, D * (t % 2):D * (t % 2) + D],
                                    lambda a, kc: OT[a][:, kc, P * t:P * t + P],
                                    lambda z, kc: WOUT[z][:, kc, :], passed)
                    mm.then_inc(s_opf, 1)
                    reader[n] = (s_y, 2, i + 1, dr)
                elif name == "x1t":
                    i = step[1]
                    pe.wait_ge(s_x1, 4 * r + 4)
                    for t in range(TB):
                        passed()
                        mm = pe.transpose(G[:, P * t:P * t + P], X1[:, t, P * i:P * i + P], IDN[:, :])
                    mm.then_inc(s_x1tf, 1)
                    reader[n] = (s_x1l, 2, i + 1, dr)
                elif name == "f1":
                    hf, p = step[1], step[2]
                    pe.wait_ge(s_x1h, 2 * r + 2)
                    pe.wait_ge(s_x1l, 2 * r + 2)
                    if first and hf == 0 and p == 0:
                        pe.wait_ge(s_quant, 4)
                        pe.wait_ge(s_wsplit_h, 3)
                        pe.wait_ge(s_b1, 16)
                    for k, f in enumerate((2 * p, 2 * p + 1)):
                        ps = G[:, 256 * k:256 * k + 256]
                        passed()
                        pe.matmul(ps, B1[:, P * f:P * f + P], ONES2[:, :], start=True, stop=False)
                        for kc in range(KC):
                            for a in range(2):
                                passed()
                                mm = pe.matmul(ps, W1Q[:, kc, P * f:P * f + P],
                                               X1T[a][:, kc, 256 * hf:256 * hf + 256],
                                               start=False, stop=(kc == KC - 1 and a == 1))
                    mm.then_inc(s_f1f, 1)
                    reader[n] = (s_hl, 8, 4 * hf + p + 1, dr)
                elif name == "f2":
                    hf = step[1]
                    pe.wait_ge(s_hh, 8 * r + 4 * hf + 4)
                    pe.wait_ge(s_hl, 8 * r + 4 * hf + 4)
                    for t in range(2):
                        for f in range(FC):
                            for a in range(2):
                                passed()
                                mm = pe.matmul(G[:, D * t:D * t + D], HID[a][:, f, P * t:P * t + P],
                                               W2Q[:, f, :], start=(f == 0 and a == 0),
                                               stop=(f == FC - 1 and a == 1))
                    mm.then_inc(s_f2f, 1)
                    reader[n] = (s_z, 2, hf + 1, dr)

            def step(b, at):
                attn = stages(at)[0]
                entry = list(reader)
                for v in range(QUADS):
                    if at == -1 and v == 2:
                        weight_totals()
                    q = max_quad(v, at)
                    for step, woven in zip(SIDE[v], WOVEN[v]):
                        places = [0]

                        def units(until):
                            for place, kind, i in woven:
                                if places[0] <= place < until:
                                    if kind == "scores" and attn:
                                        scores(b, v, i, at)
                                    elif kind == "max" and q is not None:
                                        max_scores(b + q[0], q[1], i, at == -1)
                            places[0] = until

                        def passed():
                            units(places[0] + 1)

                        row = row_of(v, step, at)
                        if row is not None and name_of(step) in COST:
                            side_work(v, step, b, *row, at, passed)
                        units(1000)
                for n in range(N_SHARED):
                    if reader[n] is not None:
                        reader[n] = reader[n][:3] + (reader[n][3] - 1,)
                assert at is not None or reader == entry

            steps(pe, step)

        @block.scalar
        def _(act):
            act.wait_ge(s_wq, 16)
            act.activation(WQKV[0][:, :, :], WQRAW, ACT.Identity).then_inc(s_wsplit_h, 1)

            def weight_sums(i):
                if i == 0:
                    act.wait_ge(s_w1, 32)
                    for k in range(2):
                        act.activation(W1Q[:, k, :], W1RAW[k], ACT.Abs, accum_out=ABS[:, 2 * k:2 * k + 1]) \
                            .then_inc(s_abs, 1)
                else:
                    act.wait_ge(s_w2, 16)
                    raw = PRF[:, W2AT:W2AT + 2 * HALF_W]
                    act.activation(W2Q[:, :, :].rearrange(FLAT), raw, ACT.Abs, accum_out=ABS[:, 1:2]).then_inc(s_abs, 1)

            def other_weights():
                act.wait_ge(s_wo, 32)
                act.activation(WOUT[0][:, :, :], WORAW, ACT.Identity).then_inc(s_wsplit_h, 1)
                act.activation(B1[0:1, :], B1R, ACT.Identity).then_inc(s_wsplit_h, 1)

            def exp(b, v, i, at):
                q = 4 * b + v
                g, u = i // 3, i % 3
                if i == 0 and not (at == 0 and v < 2):
                    act.wait_ge(s_pvf, q - 1)
                if at == 0 and v == 1 and i == 0:
                    act.wait_ge(s_wsplit_l, 3)
                    act.wait_ge(s_quant, 2)
                first, n = ((0, 384), (768, 384), (1536, 512))[u]
                lo = first + n * (g % 2)
                act.wait_ge(s_stf, 12 * q + i + 1)
                act.activation(PR[:, v % 2, g // 2, lo:lo + n], PST[i % 2][:, 0:n], ACT.Exp, scale=SCALE) \
                    .then_inc(s_exp, 1)

            def side_work(v, step, b, dr, vq, at):
                name = name_of(step)
                r = b + dr
                first = at is not None and at + dr == 0
                n = BANK.get((v, step))
                G = PG[n] if n is not None else None
                if name == "xs":
                    kc = step[1]
                    act.wait_ge(s_x, 16 * r + 16)
                    if not first:
                        act.wait_ge(s_qkf, 4 * r)
                        act.wait_ge(s_vf, 2 * r)
                    act.activation(XT[0][:, kc, :], XRAW[:, kc, :], ACT.Identity).then_inc(s_xh, 1)
                elif name == "qk":
                    j = step[1]
                    act.wait_ge(s_qkf, 4 * r + j + 1)
                    if first and j == 0:
                        act.wait_ge(s_small, 32)
                    if not first:
                        act.wait_ge(s_stk[2 * (j // 2)], 96 * r)
                        act.wait_ge(s_stk[2 * (j // 2) + 1], 96 * r)
                    act.activation(QK[j][0][:, :], G[:, :], ACT.Identity, bias=BQK[:, j:j + 1]) \
                        .then_inc(s_qkh, 1)
                elif name == "vp":
                    i = step[1]
                    act.wait_ge(s_vf, 2 * r + i + 1)
                    if i == 0 and not first:
                        act.wait_ge(s_va, 4 * r)
                    act.activation(VN[:, 2 * i:2 * i + 2, :].rearrange("p t d -> p (t d)"), G[:, :],
                                   ACT.Identity).then_inc(s_v, 1)
                elif name == "nmt":
                    q = 4 * r + vq
                    act.wait_ge(s_nmtf, q + 1)
                    if not (first and vq < 2):
                        act.wait_ge(s_nmin[(vq + 2) % 4], 16 * r + (0 if vq < 2 else 16))
                    act.activation(NMT[:, vq % 2], G[0:8 * NB, 0:W], ACT.Identity).then_inc(s_nmt, 1)
                elif name == "pvb":
                    q = 4 * r + vq
                    act.wait_ge(s_pvf, q + 1)
                    if not (first and vq == 0):
                        act.wait_ge(s_utf, q)
                    act.activation(U[:, :], G[:, :], ACT.Identity).then_inc(s_u, 1)
                elif name == "ot":
                    i = step[1]
                    act.wait_ge(s_otf, 2 * r + i + 1)
                    if not first:
                        act.wait_ge(s_opf, 2 * r)
                    act.activation(OT[0][:, i, :], G[:, :], ACT.Identity, bias=BV[:, i:i + 1]).then_inc(s_oth, 1)
                elif name == "x1" and step[1] % 2 == 0:
                    t = step[1]
                    act.wait_ge(s_nmr, 2 * r + 2)
                    if not first:
                        act.wait_ge(s_od, 32 * r)
                    act.activation(X1[:, t, :], Y[:, t, :], ACT.Identity, bias=NMR1[:, t:t + 1],
                                   scale=RS1[:, t:t + 1]).then_inc(s_x1, 1)
                elif name == "x1t":
                    i = step[1]
                    act.wait_ge(s_x1tf, 2 * r + i + 1)
                    if not first:
                        act.wait_ge(s_f1f, 8 * r)
                    act.activation(X1T[0][:, i, :], G[:, :], ACT.Identity).then_inc(s_x1h, 1)
                elif name == "f1":
                    hf, p = step[1], step[2]
                    act.wait_ge(s_f1f, 8 * r + 4 * hf + p + 1)
                    if not (first and hf == 0):
                        act.wait_ge(s_f2f, 2 * r + hf)
                    act.activation(HID[0][:, 2 * p:2 * p + 2, :].rearrange("p f t -> p (f t)"), G[:, :],
                                   ACT.Relu).then_inc(s_hh, 1)

            def step(b, at):
                attn = stages(at)[0]
                for v in range(QUADS):
                    if at == -1 and v == 0:
                        weight_sums(0)
                    for k, (step, woven) in enumerate(zip(SIDE[v], WOVEN[v])):
                        if at == -1 and v == 0 and k == 1:
                            weight_sums(1)
                            other_weights()
                        for _, kind, i in woven:
                            if kind == "scores" and attn:
                                exp(b, v, i, at)
                        row = row_of(v, step, at)
                        if row is not None:
                            side_work(v, step, b, *row, at)

            steps(act, step)

        @block.vector
        def _(dve):
            dve.memset(ONES[:, :], 1.0).then_inc(s_const, 1)
            dve.memset(VAUG[:, :, :, :, :], 1.0).then_inc(s_const, 1)
            dve.wait_ge(s_wsplit_h, 1)
            dve.tensor_tensor(WQKV[1][:, :, :], WQRAW, WQKV[0][:, :, :].bitcast(F32), ALU.subtract) \
                .then_inc(s_wsplit_l, 1)

            def other_weights():
                dve.wait_ge(s_wsplit_h, 3)
                dve.tensor_tensor(WOUT[1][:, :, :], WORAW, WOUT[0][:, :, :].bitcast(F32), ALU.subtract) \
                    .then_inc(s_wsplit_l, 1)
                dve.tensor_tensor(Y[0:1, :, :].rearrange("p t d -> p (t d)"), B1R, B1[0:1, :].bitcast(F32),
                                  ALU.subtract).then_inc(s_wsplit_l, 1)

            def thresholds():
                dve.wait_ge(s_gam, 1)
                dve.tensor_scalar(THR[:, 0:2], PMX[0][:, 0:2], 1.0 / (D * FF), EPS, ALU.mult, ALU.add) \
                    .then_inc(s_dconst, 1)
                dve.wait_ge(s_dconst, 1)
                dve.tensor_scalar(THR[:, 2:4], THR[:, 0:2], -0.5, None, ALU.mult).then_inc(s_dconst, 1)
                dve.wait_ge(s_dconst, 2)
                dve.tensor_scalar(THR[:, 0:2], THR[:, 0:2], 0.5, None, ALU.mult).then_inc(s_thr, 1)

            def quantise(n):
                i, k = QUANTISED[n]
                raw = (W1RAW, W2RAW)[i][k]
                ternary = (W1Q, W2Q)[i][:, :, :].rearrange(FLAT)[:, HALF_W * k:HALF_W * (k + 1)]
                dve.wait_ge(s_thr, 1)
                if n > 0:
                    dve.wait_ge(s_quant, n)
                dve.tensor_scalar(QTMP, raw, THR[:, 2 + i:3 + i], None, ALU.is_lt).then_inc(s_dconst, 1)
                dve.wait_ge(s_dconst, 3 + n)
                dve.scalar_tensor_tensor(ternary, raw, THR[:, i:i + 1], QTMP.bitcast(F32), ALU.is_gt,
                                         ALU.subtract).then_inc(s_quant, 1)

            def row_max(r, v, i, first):
                g, u = i // 3, i % 3
                if i == 0 and not (first and v == 0):
                    count = in_register(dve, 4 * r + v)
                    dve.wait_ge(s_const, CONSTANTS)
                    dve.wait_ge(s_nm, count)
                count = in_register(dve, 12 * (4 * r + v) + i + 1)
                dve.wait_ge(s_const, CONSTANTS)
                dve.wait_ge(s_mxf, count)
                for m in BLOCKS[u]:
                    n = PCOL[m][3]
                    ps = PMX[i % N_MAX][:, n * (m == 0):n * (m == 0) + n]
                    band = BAND[:, W:3 * W] if m == 0 else BAND[:, 0:n]
                    mx = dve.tensor_tensor_reduce(ps, ps, band, 1.0, -3e38, ALU.add, ALU.max, RMAX[:, g, m:m + 1])
                mx.then_inc(s_mxr, 1)

            def neg_max(r, v, first):
                q = 4 * r + v
                dve.wait_ge(s_mxr, 12 * q + 12)
                if not (first and v == 0):
                    dve.wait_ge(s_nmtf, q)
                dve.tensor_scalar(NM[:, 0].bitcast(F32R), RMAX[:, :, :], -1.0, None, ALU.mult) \
                    .then_inc(s_nmh, 1)
                dve.wait_ge(s_nmh, q + 1)
                dve.scalar_tensor_tensor(NM[:, 1], RMAX[:, :, :], -1.0, NM[:, 0], ALU.mult,
                                         ALU.subtract).then_inc(s_nm, 1)

            def side_work(v, step, b, dr, vq, at):
                name = name_of(step)
                r = b + dr
                first = at is not None and at + dr == 0
                n = BANK.get((v, step))
                G = PG[n] if n is not None else None
                if step == ("xs", 1) and first:
                    dve.wait_ge(s_xh, 2)
                    dve.tensor_tensor(XT[1][:, :, :], XRAW[:, :, :], XT[0][:, :, :].bitcast(F32),
                                      ALU.subtract).then_inc(s_xl, 1)
                elif name == "qk":
                    j = step[1]
                    dve.wait_ge(s_qkh, 4 * r + j + 1)
                    dve.scalar_tensor_tensor(QK[j][1][:, :], G[:, :], BQK[:, j:j + 1],
                                             QK[j][0][:, :].bitcast(F32), ALU.add, ALU.subtract) \
                        .then_inc(s_qkl, 1)
                elif name == "ut":
                    q = 4 * r + vq
                    dve.wait_ge(s_utf, q + 1)
                    if not (first and vq == 0):
                        dve.wait_ge(s_on, q)
                    sums = G[:, :].rearrange("p (a e) -> p a e", e=32)
                    dve.reciprocal(RC[:, :], sums[:, :, 16]).then_inc(s_rc, 1)
                    dve.wait_ge(s_rc, q + 1)
                    if vq == 0 and not first:
                        dve.wait_ge(s_otf, 2 * r)
                    dve.tensor_tensor(ON[:, :, 64 * vq:64 * vq + 64].rearrange("p t (g d) -> p t g d", g=4),
                                      sums[:, :, 0:16].rearrange("p (t g) d -> p t g d", t=TB),
                                      RC[:, :].rearrange("p (t g) -> p t g", t=TB)[:, :, :, None]
                                      .to_broadcast([P, TB, 4, DH]), ALU.mult).then_inc(s_on, 1)
                elif name == "ot":
                    i = step[1]
                    dve.wait_ge(s_oth, 2 * r + i + 1)
                    dve.scalar_tensor_tensor(OT[1][:, i, :], G[:, :], BV[:, i:i + 1], OT[0][:, i, :].bitcast(F32),
                                             ALU.add, ALU.subtract) \
                        .then_inc(s_otl, 1)
                elif name == "op":
                    i = step[1]
                    dve.wait_ge(s_opf, 2 * r + i + 1)
                    dve.wait_ge(s_xrb, r + 1)
                    y = Y[:, 2 * i:2 * i + 2, :]
                    dve.tensor_tensor(y, G[:, :].rearrange("p (t d) -> p t d", t=2), y, ALU.add) \
                        .then_inc(s_y, 1)
                elif name == "ln1":
                    if not first:
                        dve.wait_ge(s_mv2, 4 * r)
                        dve.wait_ge(s_x1, 4 * r)
                    t = step[1]
                    dve.wait_ge(s_y, 2 * r + 1 + t // 2)
                    dve.bn_stats(ST[:, t, :], Y[:, t, :]).then_inc(s_st1, 1)
                    for t in {0: (), 3: (2, 3)}.get(t, (t - 1,)):
                        count = in_register(dve, 4 * r + 1 + t)
                        dve.wait_ge(s_const, CONSTANTS)
                        dve.wait_ge(s_st1, count)
                        dve.bn_aggr(MV1[:, t, :], ST[:, t, :]).then_inc(s_mv1, 1)
                elif name == "x1" and step[1] % 2 == 1:
                    t = step[1]
                    dve.wait_ge(s_rs1, r + 1)
                    if not first:
                        dve.wait_ge(s_od, 32 * r)
                    dve.tensor_scalar(X1[:, t, :], Y[:, t, :], MV1[:, t, 0:1], RS1[:, t:t + 1],
                                      ALU.subtract, ALU.mult).then_inc(s_x1, 1)
                elif name == "x1t":
                    i = step[1]
                    dve.wait_ge(s_x1h, 2 * r + i + 1)
                    dve.tensor_tensor(X1T[1][:, i, :], G[:, :], X1T[0][:, i, :].bitcast(F32), ALU.subtract) \
                        .then_inc(s_x1l, 1)
                elif name == "f1":
                    hf, p = step[1], step[2]
                    dve.wait_ge(s_hh, 8 * r + 4 * hf + p + 1)
                    pair = [h[:, 2 * p:2 * p + 2, :].rearrange("p f t -> p (f t)") for h in HID]
                    dve.scalar_tensor_tensor(pair[1], G[:, :], 0.0, pair[0].bitcast(F32), ALU.max,
                                             ALU.subtract).then_inc(s_hl, 1)
                elif name == "f2":
                    hf = step[1]
                    dve.wait_ge(s_f2f, 2 * r + hf + 1)
                    dve.wait_ge(s_x1b, r + 1)
                    z = X1[:, 2 * hf:2 * hf + 2, :]
                    dve.tensor_tensor(z, G[:, :].rearrange("p (t d) -> p t d", t=2), z, ALU.add) \
                        .then_inc(s_z, 1)
                elif name == "ln2":
                    t, hf = step[1], step[1] // 2
                    dve.wait_ge(s_mv1, 4 * r + 4)
                    if not first:
                        dve.wait_ge(s_o, 4 * r)
                    dve.wait_ge(s_z, 2 * r + hf + 1)
                    dve.bn_stats(ST[:, t, :], X1[:, t, :]).then_inc(s_st2, 1)
                    for t in ((t - 1, t) if t % 2 else ()):
                        count = in_register(dve, 4 * r + 1 + t)
                        dve.wait_ge(s_const, CONSTANTS)
                        dve.wait_ge(s_st2, count)
                        dve.bn_aggr(MV2[:, t, :], ST[:, t, :]).then_inc(s_mv2, 1)
                    if at == B and t % 2:
                        dve.wait_ge(s_rs2, 2 * r + hf + 1)
                        for t in (2 * hf, 2 * hf + 1):
                            dve.tensor_scalar(X1[:, t, :], X1[:, t, :], MV2[:, t, 0:1], RS2[:, t:t + 1],
                                              ALU.subtract, ALU.mult).then_inc(s_o, 1)

            def step(b, at):
                for v in range(QUADS):
                    if at == -1 and v == 1:
                        other_weights()
                    if at == -1 and v == 2:
                        thresholds()
                        quantise(0)
                    if at == 0 and v < 3:
                        quantise(v + 1)
                    q = max_quad(v, at)
                    for kind, what in dve_order(v):
                        if kind == "max":
                            if q is not None:
                                row_max(b + q[0], q[1], what, at == -1)
                                if what == UNITS - 1:
                                    neg_max(b + q[0], q[1], at == -1)
                        else:
                            row = row_of(v, what, at)
                            if row is not None:
                                side_work(v, what, b, *row, at)

            steps(dve, step)

        @block.gpsimd
        def _(pool):
            pool.memset(IDN[:, :], 0.0).then_inc(s_blank, 1)
            pool.memset(BAND[:, :], 0.0).then_inc(s_blank, 1)
            pool.wait_ge(s_blank, 2)
            pool.affine_select(out=IDN[:, :], in_=IDN[:, :], compare_op=ALU.not_equal, fill=1.0, base=0,
                               pattern=[[-1, P]], channel_multiplier=1).then_inc(s_const, 1)
            pool.affine_select(out=BAND[:, 0:W], in_=BAND[:, 0:W], compare_op=ALU.is_ge, fill=MASKED, base=0,
                               pattern=[[1, W]], channel_multiplier=-1).then_inc(s_const, 1)
            pool.affine_select(out=BAND[:, 2 * W:3 * W], in_=BAND[:, 2 * W:3 * W], compare_op=ALU.is_ge,
                               fill=MASKED, base=0, pattern=[[-1, W]], channel_multiplier=1) \
                .then_inc(s_const, 1)

            pool.memset(HALF[:, :], -0.5).then_inc(s_const, 1)
            pool.memset(ONES2[:, :].bitcast(F32), 1.0).then_inc(s_const, 1)
            pool.memset(SK[:, :, :].bitcast(F32), 1.0).then_inc(s_const, 1)
            pool.wait_ge(s_const, CONSTANTS)

            def mask(b, v, g):
                count = in_register(pool, 3 * (16 * b + 4 * v + g) + 3)
                pool.wait_ge(s_const, CONSTANTS)
                pool.wait_ge(s_exp, count)
                pr = PR[:, v % 2, g // 2, :]
                inner = pr[:, 0:1536].rearrange("p (m w) -> p m w", w=384)
                outer = pr[:, 1536:2560].rearrange("p (h w) -> p h w", w=512)
                for pr_before, n in ((inner[:, :, 0:W], 4), (outer[:, :, 0:W], 2)):
                    pool.affine_select(out=pr_before, in_=pr_before, compare_op=ALU.is_ge, fill=0.0, base=0,
                                       pattern=[[0, n], [1, W]], channel_multiplier=-1)
                for pr_after, n in ((inner[:, :, 2 * W:3 * W], 4), (outer[:, :, 3 * W:4 * W], 2)):
                    last = pool.affine_select(out=pr_after, in_=pr_after, compare_op=ALU.is_ge, fill=0.0, base=0,
                                              pattern=[[0, n], [-1, W]], channel_multiplier=1)
                last.then_inc(s_mask, 1)

            def v_in_place(r, v, first):
                count = in_register(pool, 4 * (r - 1) + v + 1)
                made = in_register(pool, 2 * r + 2)
                pool.wait_ge(s_const, CONSTANTS)
                pool.wait_ge(s_v, made)
                if not first:
                    pool.wait_ge(s_pvf, count)
                pool.tensor_copy(VAUG[:, v, :, :, 0:DH],
                                 VN[:, :, 64 * v:64 * v + 64].rearrange("p t (g d) -> p t g d", g=4)) \
                    .then_inc(s_va, 1)

            def side_work(v, step, b, dr, vq, at):
                name = name_of(step)
                r = b + dr
                first = at is not None and at + dr == 0
                if step == ("xs", 1) and not first:
                    pool.wait_ge(s_xh, 2 * r + 2)
                    pool.tensor_tensor(XT[1][:, :, :], XRAW[:, :, :], XT[0][:, :, :].bitcast(F32),
                                       ALU.subtract).then_inc(s_xl, 1)
                elif name == "xr":
                    pool.wait_ge(s_xr, 16 * r + 16)
                    if first:
                        pool.wait_ge(s_b2, 32)
                    pool.tensor_tensor(Y[:, :, :], Y[:, :, :], BOUT[:, None, :].to_broadcast([P, TB, D]),
                                       ALU.add).then_inc(s_xrb, 1)
                elif step == ("ln1", 3):
                    count = in_register(pool, 4 * r + 4)
                    pool.wait_ge(s_const, CONSTANTS)
                    pool.wait_ge(s_mv1, count)
                    pool.tensor_scalar(VE[:, :], MV1[:, :, 1], 1.0, EPS, ALU.mult, ALU.add).then_inc(s_ve, 1)
                    pool.wait_ge(s_ve, 3 * r + 1)
                    pool.tensor_tensor(RS1[:, :], VE[:, :], HALF[:, :], ALU.pow).then_inc(s_rs1, 1)
                    pool.tensor_scalar(NEG1[:, :], MV1[:, :, 0], -1.0, None, ALU.mult).then_inc(s_nmr, 1)
                    pool.wait_ge(s_rs1, r + 1)
                    pool.wait_ge(s_nmr, 2 * r + 1)
                    pool.tensor_tensor(NMR1[:, :], NEG1[:, :], RS1[:, :], ALU.mult).then_inc(s_nmr, 1)
                elif name == "x1t" and step[1] == 1:
                    pool.wait_ge(s_x1tf, 2 * r + 2)
                    pool.tensor_tensor(X1[:, :, :], X1[:, :, :], B2[:, None, :].to_broadcast([P, TB, D]),
                                       ALU.add).then_inc(s_x1b, 1)
                elif name == "ln2" and step[1] % 2 == 1:
                    hf = step[1] // 2
                    two = slice(2 * hf, 2 * hf + 2)
                    count = in_register(pool, 4 * r + 2 * hf + 2)
                    pool.wait_ge(s_const, CONSTANTS)
                    pool.wait_ge(s_mv2, count)
                    pool.tensor_scalar(VE[:, two], MV2[:, two, 1], 1.0, EPS, ALU.mult, ALU.add).then_inc(s_ve, 1)
                    pool.wait_ge(s_ve, 3 * r + 2 + hf)
                    pool.tensor_tensor(RS2[:, two], VE[:, two], HALF[:, two], ALU.pow).then_inc(s_rs2, 1)
                    if at == B:
                        return
                    count = in_register(pool, 2 * r + hf + 1)
                    pool.wait_ge(s_const, CONSTANTS)
                    pool.wait_ge(s_rs2, count)
                    for t in (2 * hf, 2 * hf + 1):
                        pool.tensor_scalar(X1[:, t, :], X1[:, t, :], MV2[:, t, 0:1], RS2[:, t:t + 1],
                                           ALU.subtract, ALU.mult).then_inc(s_o, 1)

            def step(b, at):
                attn = stages(at)[0]
                for v in range(QUADS):
                    if v == 0 and attn:
                        for vq in range(3):
                            v_in_place(b, vq, at == 0)
                    for step, woven in zip(SIDE[v], WOVEN[v]):
                        if attn:
                            for _, kind, i in woven:
                                if kind == "scores" and i in (5, 11):
                                    mask(b, v, i // 3)
                            if v == 0 and step == "ut":
                                v_in_place(b, 3, at == 0)
                        row = row_of(v, step, at)
                        if row is not None:
                            side_work(v, step, b, *row, at)

            steps(pool, step)


def kernel(L0_attn_x, L0_attn_Wqkv, L0_attn_bqkv, L0_attn_Wout, L0_attn_bout, L0_ffn_W1, L0_ffn_b1,
           L0_ffn_W2, L0_ffn_b2):
    import numpy as np
    from concourse import bacc
    from concourse.bass_utils import run_bass_kernel_spmd

    x = np.ascontiguousarray(L0_attn_x)
    wqkv = np.asarray(L0_attn_Wqkv)
    bqkv = np.asarray(L0_attn_bqkv)
    order = np.arange(2 * D).reshape(2, 2, 2, 4, DH).transpose(1, 0, 2, 4, 3).reshape(-1)
    arrays = {
        "x": x,
        "xT": np.ascontiguousarray(x.transpose(0, 2, 1)),
        "wqkv": np.ascontiguousarray(np.concatenate([wqkv[:, order], wqkv[:, 2 * D:]], axis=1)),
        "bqk": np.ascontiguousarray(bqkv[order].reshape(4, P).T),
        "bv": np.ascontiguousarray(bqkv[2 * D:].reshape(KC, P).T),
        "wout": np.ascontiguousarray(L0_attn_Wout),
        "bout": np.ascontiguousarray(L0_attn_bout),
        "w1T": np.ascontiguousarray(np.asarray(L0_ffn_W1).T),
        "b1": np.ascontiguousarray(L0_ffn_b1),
        "w2T": np.ascontiguousarray(np.asarray(L0_ffn_W2).T),
        "b2": np.ascontiguousarray(L0_ffn_b2),
    }
    nc = bacc.Bacc("TRN2", target_bir_lowering=False, num_devices=1)
    aps = {n: nc.dram_tensor(f"in_{n}", a.shape, mybir.dt.from_np(a.dtype), kind="ExternalInput").ap()
           for n, a in arrays.items()}
    out = nc.dram_tensor("out", (B, S, D), F32, kind="ExternalOutput").ap()
    postln_layer(nc, out=out, **aps)
    result = run_bass_kernel_spmd(nc, [{f"in_{n}": a for n, a in arrays.items()}], core_ids=[0])
    return result.results[0]["out"]
```
